# Optimizing a Trainium2 kernel written in Bass

```python
import numpy as np
import jax
import jax.numpy as jnp

def _softmax(x, axis=-1):
    return jax.nn.softmax(x, axis=axis)

def _gelu(x):
    return jax.nn.gelu(x, approximate=True)

def _silu(x):
    return jax.nn.silu(x)

def _sigmoid(x):
    return jax.nn.sigmoid(x)

def _layernorm(x, axis=-1, eps=1e-05):
    m = jnp.mean(x, axis=axis, keepdims=True)
    v = jnp.var(x, axis=axis, keepdims=True)
    return (x - m) / jnp.sqrt(v + eps)

def _scatter_add(tgt, idx, src, axis=0):
    return tgt.at[idx].add(src)

def _segment_sum(src, seg, n):
    return jax.ops.segment_sum(src, seg, n)
kernel_name = 'mk_gnn_resnorm_d4_gnn_r32_6b8b95'

def setup_inputs(seed: int=0):
    np.random.seed(seed)
    _w = jnp.asarray

    def _rec_inputs():
        import jax
        import jax.numpy as jnp
        _gk = jax.random.key(seed)
        x = -0.000202 + 1 * jax.random.normal(jax.random.fold_in(_gk, 1), (3125, 64), jnp.float32)
        src = jax.random.randint(jax.random.fold_in(_gk, 2), (100000,), 0, 3125, jnp.int32)
        dst = jnp.minimum((3125 * jax.random.uniform(jax.random.fold_in(_gk, 3), (100000,)) ** 2.0).astype(jnp.int32), 99999)
        _o = jnp.argsort(dst, stable=True)
        src = src[_o]
        dst = dst[_o]
        edge_attr_16 = 0.000196303 + 1.00016 * jax.random.normal(jax.random.fold_in(_gk, 12), (100000, 16), jnp.float32)
        edge_attr_8 = -0.000153872 + 1.00011 * jax.random.normal(jax.random.fold_in(_gk, 13), (100000, 8), jnp.float32)
        return (x, src, dst, edge_attr_16, edge_attr_8)
    x, src, dst, edge_attr_16, edge_attr_8 = _rec_inputs()

    def _L0_gnn_setup():
        import jax, jax.numpy as jnp
        import numpy as np
        N_NODES = 3125
        N_EDGES = 50000
        IN_CH = 64
        OUT_CH = 64
        EDGE_DIM = 16
        key = jax.random.key(seed)
        ks = jax.random.split(key, 8)
        x = jax.random.normal(ks[0], (N_NODES, IN_CH), dtype=jnp.float32)
        edge_index = jax.random.randint(ks[1], (2, N_EDGES), 0, N_NODES, dtype=jnp.int64)
        edge_attr = jax.random.normal(ks[2], (N_EDGES, EDGE_DIM), dtype=jnp.float32)
        W_l = jax.random.normal(ks[3], (IN_CH, OUT_CH), dtype=jnp.float32) / np.sqrt(IN_CH)
        b_l = jnp.zeros((OUT_CH,), dtype=jnp.float32)
        W_r = jax.random.normal(ks[4], (IN_CH, OUT_CH), dtype=jnp.float32) / np.sqrt(IN_CH)
        W_e = jax.random.normal(ks[5], (EDGE_DIM, OUT_CH), dtype=jnp.float32) / np.sqrt(EDGE_DIM)
        b_e = jax.random.normal(ks[6], (OUT_CH,), dtype=jnp.float32) * 0.01
        return {'x': x, 'edge_index': edge_index, 'edge_attr': edge_attr, 'W_l': W_l, 'b_l': b_l, 'W_r': W_r, 'W_e': W_e, 'b_e': b_e}
    _L0_gnn_all = _L0_gnn_setup()
    _L0_gnn_in = {k: v for k, v in _L0_gnn_all.items() if k in ('W_l', 'b_l', 'W_r', 'W_e', 'b_e')}
    del _L0_gnn_all

    def _L1_gnn_setup():
        import jax, jax.numpy as jnp
        import numpy as np
        N = 50000
        E = 12500
        F_IN = 64
        HID = 128
        OUT = 64
        HEADS = 4
        NEG_SLOPE = 0.2
        BN_EPS = 1e-05

        def _gat_conv(x, src, dst, W, a_src, a_dst, bias, heads, ch):
            n = x.shape[0]
            h = (x @ W).reshape(n, heads, ch)
            alpha_src = jnp.sum(h * a_src, axis=-1)
            alpha_dst = jnp.sum(h * a_dst, axis=-1)
            e = jax.nn.leaky_relu(alpha_src[src] + alpha_dst[dst], NEG_SLOPE)
            m = jax.lax.stop_gradient(jax.ops.segment_max(e, dst, num_segments=n))
            ex = jnp.exp(e - m[dst])
            den = jax.ops.segment_sum(ex, dst, num_segments=n)
            alpha = ex / den[dst]
            msg = h[src] * alpha[..., None]
            out = jax.ops.segment_sum(msg, dst, num_segments=n)
            return jnp.mean(out, axis=1) + bias

        def _batch_norm(x, gamma, beta):
            mu = jnp.mean(x, axis=0)
            var = jnp.mean(jnp.square(x - mu), axis=0)
            return (x - mu) * jax.lax.rsqrt(var + BN_EPS) * gamma + beta
        key = jax.random.key(seed)
        ks = jax.random.split(key, 20)
        f = lambda k, shape, s=0.1: jax.random.normal(k, shape, jnp.float32) * s
        return {'x': jax.random.normal(ks[0], (N, F_IN), jnp.float32), 'edge_index': jax.random.randint(ks[1], (2, E), 0, N, jnp.int32), 'W1': f(ks[2], (F_IN, HEADS * HID)), 'as1': f(ks[3], (HEADS, HID)), 'ad1': f(ks[4], (HEADS, HID)), 'b1': f(ks[5], (HID,)), 'g1': jnp.ones((HID,), jnp.float32), 'be1': jnp.zeros((HID,), jnp.float32), 'W2': f(ks[6], (HID, HEADS * HID)), 'as2': f(ks[7], (HEADS, HID)), 'ad2': f(ks[8], (HEADS, HID)), 'b2': f(ks[9], (HID,)), 'g2': jnp.ones((HID,), jnp.float32), 'be2': jnp.zeros((HID,), jnp.float32), 'W3': f(ks[10], (HID, 1 * OUT)), 'as3': f(ks[11], (1, OUT)), 'ad3': f(ks[12], (1, OUT)), 'b3': f(ks[13], (OUT,))}
    _L1_gnn_all = _L1_gnn_setup()
    _L1_gnn_in = {k: v for k, v in _L1_gnn_all.items() if k in ('W1', 'as1', 'ad1', 'b1', 'g1', 'be1', 'W2', 'as2', 'ad2', 'b2', 'g2', 'be2', 'W3', 'as3', 'ad3', 'b3')}
    del _L1_gnn_all

    def _L2_gnn_setup():
        import jax, jax.numpy as jnp
        import numpy as np
        NUM_NODES = 3125
        D_IN = 64
        D_OUT = 64
        NUM_EDGES = 37500
        key = jax.random.key(seed)
        k1, k2, k3, k4 = jax.random.split(key, 4)
        features = jax.random.normal(k1, (NUM_NODES, D_IN), dtype=jnp.float32)
        edge_index = jax.random.randint(k2, (2, NUM_EDGES), 0, NUM_NODES, dtype=jnp.int64)
        W = jax.random.normal(k3, (2 * D_IN, D_OUT), dtype=jnp.float32) / np.sqrt(2 * D_IN)
        b = jax.random.normal(k4, (D_OUT,), dtype=jnp.float32) * 0.01
        return {'features': features, 'edge_index': edge_index, 'W': W, 'b': b}
    _L2_gnn_all = _L2_gnn_setup()
    _L2_gnn_in = {k: v for k, v in _L2_gnn_all.items() if k in ('W', 'b')}
    del _L2_gnn_all

    def _L3_gnn_setup():
        import jax, jax.numpy as jnp
        import numpy as np
        N_NODES = 625
        N_EDGES = 31250
        C = 64
        H = 64
        N_BASIS = 8
        key = jax.random.key(seed)
        ks = jax.random.split(key, 10)

        def glorot(k, shape):
            fan_in, fan_out = (shape[0], shape[1])
            lim = np.sqrt(6.0 / (fan_in + fan_out)).astype(np.float32)
            return jax.random.uniform(k, shape, jnp.float32, -lim, lim)
        return {'p': jax.random.normal(ks[0], (N_NODES, C), jnp.float32), 'idx_i': jax.random.randint(ks[1], (N_EDGES,), 0, N_NODES), 'idx_j': jax.random.randint(ks[2], (N_EDGES,), 0, N_NODES), 'basis': jax.random.normal(ks[3], (N_EDGES, N_BASIS), jnp.float32), 'pp_W': glorot(ks[4], (C, C)), 'pp_b': jnp.zeros((C,), jnp.float32), 'pi_W1': glorot(ks[5], (2 * C, H)), 'pi_b1': jnp.zeros((H,), jnp.float32), 'pi_W2': glorot(ks[6], (H, H * N_BASIS)), 'ii_W': glorot(ks[7], (H, C)), 'ii_b': jnp.zeros((C,), jnp.float32)}
    _L3_gnn_all = _L3_gnn_setup()
    _L3_gnn_in = {k: v for k, v in _L3_gnn_all.items() if k in ('pp_W', 'pp_b', 'pi_W1', 'pi_b1', 'pi_W2', 'ii_W', 'ii_b')}
    del _L3_gnn_all
    return {'x': x, 'src': src, 'dst': dst, 'edge_attr_16': edge_attr_16, 'edge_attr_8': edge_attr_8, 'L0_gnn_W_l': _L0_gnn_in['W_l'], 'L0_gnn_b_l': _L0_gnn_in['b_l'], 'L0_gnn_W_r': _L0_gnn_in['W_r'], 'L0_gnn_W_e': _L0_gnn_in['W_e'], 'L0_gnn_b_e': _L0_gnn_in['b_e'], 'L1_gnn_W1': _L1_gnn_in['W1'], 'L1_gnn_as1': _L1_gnn_in['as1'], 'L1_gnn_ad1': _L1_gnn_in['ad1'], 'L1_gnn_b1': _L1_gnn_in['b1'], 'L1_gnn_g1': _L1_gnn_in['g1'], 'L1_gnn_be1': _L1_gnn_in['be1'], 'L1_gnn_W2': _L1_gnn_in['W2'], 'L1_gnn_as2': _L1_gnn_in['as2'], 'L1_gnn_ad2': _L1_gnn_in['ad2'], 'L1_gnn_b2': _L1_gnn_in['b2'], 'L1_gnn_g2': _L1_gnn_in['g2'], 'L1_gnn_be2': _L1_gnn_in['be2'], 'L1_gnn_W3': _L1_gnn_in['W3'], 'L1_gnn_as3': _L1_gnn_in['as3'], 'L1_gnn_ad3': _L1_gnn_in['ad3'], 'L1_gnn_b3': _L1_gnn_in['b3'], 'L2_gnn_W': _L2_gnn_in['W'], 'L2_gnn_b': _L2_gnn_in['b'], 'L3_gnn_pp_W': _L3_gnn_in['pp_W'], 'L3_gnn_pp_b': _L3_gnn_in['pp_b'], 'L3_gnn_pi_W1': _L3_gnn_in['pi_W1'], 'L3_gnn_pi_b1': _L3_gnn_in['pi_b1'], 'L3_gnn_pi_W2': _L3_gnn_in['pi_W2'], 'L3_gnn_ii_W': _L3_gnn_in['ii_W'], 'L3_gnn_ii_b': _L3_gnn_in['ii_b']}

def reference(x, src, dst, edge_attr_16, edge_attr_8, L0_gnn_W_l, L0_gnn_b_l, L0_gnn_W_r, L0_gnn_W_e, L0_gnn_b_e, L1_gnn_W1, L1_gnn_as1, L1_gnn_ad1, L1_gnn_b1, L1_gnn_g1, L1_gnn_be1, L1_gnn_W2, L1_gnn_as2, L1_gnn_ad2, L1_gnn_b2, L1_gnn_g2, L1_gnn_be2, L1_gnn_W3, L1_gnn_as3, L1_gnn_ad3, L1_gnn_b3, L2_gnn_W, L2_gnn_b, L3_gnn_pp_W, L3_gnn_pp_b, L3_gnn_pi_W1, L3_gnn_pi_b1, L3_gnn_pi_W2, L3_gnn_ii_W, L3_gnn_ii_b):
    import jax
    import jax.numpy as jnp

    def _L0_gnn_ref(x, edge_index, edge_attr, W_l, b_l, W_r, W_e, b_e):
        import jax, jax.numpy as jnp
        import numpy as np
        N_NODES = 3125
        N_EDGES = 50000
        IN_CH = 64
        OUT_CH = 64
        EDGE_DIM = 16
        N = x.shape[0]
        row, col = (edge_index[0], edge_index[1])
        x_j = x[row]
        agg = jax.ops.segment_sum(x_j, col, num_segments=N)
        cnt = jax.ops.segment_sum(jnp.ones((row.shape[0],), x.dtype), col, num_segments=N)
        mean = agg / jnp.maximum(cnt, 1.0)[:, None]
        out = mean @ W_l + b_l + x @ W_r
        e = edge_attr @ W_e + b_e
        out = out + jnp.zeros_like(out).at[col].set(e)
        return out

    def _L1_gnn_ref(x, edge_index, W1, as1, ad1, b1, g1, be1, W2, as2, ad2, b2, g2, be2, W3, as3, ad3, b3):
        import jax, jax.numpy as jnp
        import numpy as np
        N = 50000
        E = 12500
        F_IN = 64
        HID = 128
        OUT = 64
        HEADS = 4
        NEG_SLOPE = 0.2
        BN_EPS = 1e-05

        def _gat_conv(x, src, dst, W, a_src, a_dst, bias, heads, ch):
            n = x.shape[0]
            h = (x @ W).reshape(n, heads, ch)
            alpha_src = jnp.sum(h * a_src, axis=-1)
            alpha_dst = jnp.sum(h * a_dst, axis=-1)
            e = jax.nn.leaky_relu(alpha_src[src] + alpha_dst[dst], NEG_SLOPE)
            m = jax.lax.stop_gradient(jax.ops.segment_max(e, dst, num_segments=n))
            ex = jnp.exp(e - m[dst])
            den = jax.ops.segment_sum(ex, dst, num_segments=n)
            alpha = ex / den[dst]
            msg = h[src] * alpha[..., None]
            out = jax.ops.segment_sum(msg, dst, num_segments=n)
            return jnp.mean(out, axis=1) + bias

        def _batch_norm(x, gamma, beta):
            mu = jnp.mean(x, axis=0)
            var = jnp.mean(jnp.square(x - mu), axis=0)
            return (x - mu) * jax.lax.rsqrt(var + BN_EPS) * gamma + beta
        n = x.shape[0]
        loop = jnp.arange(n, dtype=edge_index.dtype)
        src = jnp.concatenate([edge_index[0], loop])
        dst = jnp.concatenate([edge_index[1], loop])
        h = _gat_conv(x, src, dst, W1, as1, ad1, b1, HEADS, HID)
        h = jax.nn.elu(_batch_norm(h, g1, be1))
        h = _gat_conv(h, src, dst, W2, as2, ad2, b2, HEADS, HID)
        h = jax.nn.elu(_batch_norm(h, g2, be2))
        return _gat_conv(h, src, dst, W3, as3, ad3, b3, 1, OUT)

    def _L2_gnn_ref(features, edge_index, W, b):
        import jax, jax.numpy as jnp
        import numpy as np
        NUM_NODES = 3125
        D_IN = 64
        D_OUT = 64
        NUM_EDGES = 37500
        num_nodes = features.shape[0]
        src, dst = (edge_index[0], edge_index[1])
        src_feats = features[src]
        neigh_sum = jax.ops.segment_sum(src_feats, dst, num_segments=num_nodes)
        degree = jax.ops.segment_sum(jnp.ones_like(dst, dtype=features.dtype), dst, num_segments=num_nodes)
        degree = jnp.clip(degree, 1.0)
        neigh_mean = neigh_sum / degree[:, None]
        combined = jnp.concatenate([features, neigh_mean], axis=-1)
        return combined @ W + b

    def _L3_gnn_ref(p, idx_i, idx_j, basis, pp_W, pp_b, pi_W1, pi_b1, pi_W2, ii_W, ii_b):
        import jax, jax.numpy as jnp
        import numpy as np
        N_NODES = 625
        N_EDGES = 31250
        C = 64
        H = 64
        N_BASIS = 8
        p1 = jnp.tanh(p @ pp_W + pp_b)
        pair = jnp.concatenate([p1[idx_i], p1[idx_j]], axis=-1)
        h = pair @ pi_W1 + pi_b1
        h = (h @ pi_W2).reshape(-1, H, N_BASIS)
        i1 = jnp.einsum('ecb,eb->ec', h, basis)
        i2 = jnp.tanh(i1 @ ii_W + ii_b)
        return p.at[idx_i].add(i2)
    edge_index = jnp.stack([src, dst])
    x = _layernorm(x + _L0_gnn_ref(x, edge_index, edge_attr_16, L0_gnn_W_l, L0_gnn_b_l, L0_gnn_W_r, L0_gnn_W_e, L0_gnn_b_e), axis=-1)
    x = _layernorm(x + _L1_gnn_ref(x, edge_index, L1_gnn_W1, L1_gnn_as1, L1_gnn_ad1, L1_gnn_b1, L1_gnn_g1, L1_gnn_be1, L1_gnn_W2, L1_gnn_as2, L1_gnn_ad2, L1_gnn_b2, L1_gnn_g2, L1_gnn_be2, L1_gnn_W3, L1_gnn_as3, L1_gnn_ad3, L1_gnn_b3), axis=-1)
    x = _layernorm(x + _L2_gnn_ref(x, edge_index, L2_gnn_W, L2_gnn_b), axis=-1)
    x = _layernorm(x + _L3_gnn_ref(x, src, dst, edge_attr_8, L3_gnn_pp_W, L3_gnn_pp_b, L3_gnn_pi_W1, L3_gnn_pi_b1, L3_gnn_pi_W2, L3_gnn_ii_W, L3_gnn_ii_b), axis=-1)
    return x

_drawn_inputs = setup_inputs


def setup_inputs(seed=0):
    import zlib

    import numpy as np

    out = dict(_drawn_inputs(seed))
    spreads = {'L0_gnn_b_l': (0.0, 0.1),
     'L1_gnn_g1': (1.0, 0.2),
     'L1_gnn_be1': (0.0, 0.508),
     'L1_gnn_g2': (1.0, 0.2),
     'L1_gnn_be2': (0.0, 0.1),
     'L3_gnn_pp_b': (0.0, 0.1),
     'L3_gnn_pi_b1': (0.0, 0.1),
     'L3_gnn_ii_b': (0.0, 0.1)}
    factors = {'L0_gnn_b_e': 7.605, 'L1_gnn_b1': 8.0, 'L1_gnn_b2': 8.0, 'L2_gnn_b': 5.448}
    for name, (base, spread) in spreads.items():
        noise = np.random.default_rng([zlib.crc32(name.encode()), seed]).standard_normal(out[name].shape)
        drawn = base * np.exp(spread * noise) if base else spread * noise
        out[name] = jnp.asarray(drawn.astype(out[name].dtype))
    for name, factor in factors.items():
        out[name] = (out[name] * factor).astype(out[name].dtype)
    return out
```

```python
from contextlib import ExitStack

import concourse.bass as bass
from concourse import mybir

F32 = mybir.dt.float32
F16 = mybir.dt.float16
BF16 = mybir.dt.bfloat16
U16 = mybir.dt.uint16
I32 = mybir.dt.int32
ALU = mybir.AluOpType
ACT = mybir.ActivationFunctionType
X_AXIS = mybir.AxisListType.X
ds = bass.ds

N = 3125
T = 125
NT = N // T
D = 64
E = 100000
NCH = E // T
PAIR = 2
NG = NCH // PAIR
BT = 5
NB = NT // BT
BW = BT * T
SLOTS = 5
HEADS = 4
NEG = 0.2
EPS = 1e-5
BANKS = 7

GAT = (("a", D, HEADS, 128), ("b", 128, HEADS, 128), ("c", 128, 1, D))


def build_gnn(nc, p, out):
    with ExitStack() as ctx:
        def sb(name, shape, dt=F32):
            return ctx.enter_context(nc.sbuf_tensor(name, shape, dt))

        def sem(name):
            return ctx.enter_context(nc.semaphore(name))

        adj = sb("adj", [T, NT * N + 3], U16)
        adj3 = adj[:, 0:NT * N].rearrange("p (j d) -> p j d", j=NT)
        scratch = sb("scratch", [128, 3200])
        hwork = sb("hwork", [128, 3225])
        rows = sb("rows", [128, 2, BW])
        aggT = sb("aggT", [128, BW])
        dent = sb("dent", [1, BW])
        acc = sb("acc", [T, BT, 128])
        X = sb("X", [T, NT, D + 1])
        edge_ids = sb("edge_ids", [T, 2, NCH], U16)
        wbuf = sb("wbuf", [128, 640])
        att = sb("att", [T, NT, 8])
        cols = sb("cols", [T, 6, NT, HEADS])
        ident = sb("ident", [128, 128])
        ones = sb("ones", [128, 128])
        small = sb("small", [128, 64])
        table = sb("table", [1, 3 * NT], I32)
        last_edge = sb("last_edge", [T, NT])
        ps = ctx.enter_context(nc.psum_tensor("ps", [128, 8, 512], F32))

        rflat = rows[:].rearrange("p a b -> p (a b)")
        hflat = hwork[:, :]
        raw_src = rflat[0:100, 0:1000].bitcast(I32).rearrange("q (k e) -> q k e", k=8)
        raw_dst = scratch[0:100, 0:1000].bitcast(I32).rearrange("q (k e) -> q k e", k=8)
        flt_src = scratch[0:100, 1000:2000].rearrange("q (k e) -> q k e", k=8)
        flt_dst = scratch[0:100, 2000:3000].rearrange("q (k e) -> q k e", k=8)
        chunk_lim = hflat[0:100, 0:16].rearrange("q (m k) -> q m k", m=2)
        gmax = hflat[0:NT, 16:416]
        gmin = hflat[0:NT, 416:816]
        rev = hflat[0:NT, 816:1216]
        fwd = hflat[0:NT, 1216:1616]
        tmpg = hflat[0:NT, 1616:2016]
        lower = hflat[0:NT, 2016:2041]
        wcol = hflat[0:NT, 2041:2051]
        eid = rflat[0:T, 0:NCH]
        onehot_src = scratch[0:T, 0:3126].bitcast(BF16).rearrange("p (c n) -> p c n", c=2)[:, :, 0:N]
        iota = hflat[0:T, 0:1563].bitcast(U16)[:, 0:N]
        zeros = hflat[0:T, 1563:1819].bitcast(BF16)
        onehot_dst = hflat[0:T, 1819:1945].bitcast(BF16).rearrange("p (c n) -> p c n", c=2)[:, :, 0:T]
        lastmax = acc[:].rearrange("p a b -> p (a b)")[:, 0:T]
        ft = scratch[:, 0:N]
        slots = scratch[0:T, 0:SLOTS * BW].rearrange("p (s d) -> p s d", s=SLOTS)
        res = hflat[0:T, 1625:3225].rearrange("p (j c) -> p j c", j=NT)
        h3 = hflat[0:T, 0:1625].rearrange("p (j c) -> p j c", j=NT)
        hid = hflat[0:T, 0:3200].rearrange("p (j c) -> p j c", j=NT)
        seen = scratch[0:T, 0:N]
        ea = hflat[0:T, 0:400].rearrange("p (j c) -> p j c", j=NT)
        eaug = hflat[0:T, 400:825].rearrange("p (j c) -> p j c", j=NT)
        eidx = hflat[0:T, 825:850].bitcast(I32)
        diag = edge_ids[:].rearrange("p a b -> p (a b)")[:, 0:2 * BW].bitcast(F32).rearrange("p (i d) -> p i d", i=BT)
        gat_out = {n: nc.dram_tensor(f"gat_out_{n}", (N, fo), F32, kind="Internal").ap() for n, _, _, fo in GAT}
        q_dram = nc.dram_tensor("q_dram", (N, D), F32, kind="Internal").ap()
        r_dram = nc.dram_tensor("r_dram", (N, D), F32, kind="Internal").ap()
        v_dram = nc.dram_tensor("v_dram", (NCH // 4, T, 4 * 128), F16, kind="Internal").ap()

        big = adj[:].bitcast(F32)

        def at(off, parts, words):
            return big[0:parts, off:off + words]

        o = 0
        basis = at(o, T, 6400).rearrange("p (t b) -> p t b", b=8); o += 6400
        idx3 = at(o, T, 1600).bitcast(I32).rearrange("p (s t) -> p s t", s=2); o += 1600
        src3 = at(o, T, 400).bitcast(U16); o += 400
        p1T = at(o, D, N); o += N
        qr = at(o, T, 3200).rearrange("p (j c) -> p j c", j=NT); o += 3200
        GS = 8
        gath = at(o, T, GS * 128).rearrange("p (s a c) -> p s a c", s=GS, a=2); o += GS * 128
        hT = at(o, D, 4 * T).rearrange("p (s e) -> p s e", s=4); o += 4 * T
        prod = at(o, T, 2 * 9 * D).rearrange("p (s b c) -> p s b c", s=2, b=9); o += 2 * 9 * D
        uval = at(o, T, 2 * 4 * D).rearrange("p (s q c) -> p s q c", s=2, q=4); o += 2 * 4 * D
        vval = at(o, T, 2 * 4 * D).rearrange("p (s q c) -> p s q c", s=2, q=4); o += 2 * 4 * D
        vsplit = at(o, T, 2 * 256).bitcast(F16).rearrange("p (s q h c) -> p s q h c", s=2, q=4, h=2); o += 512
        w2T = at(o, D, 8 * D).rearrange("p (b k) -> p b k", b=8); o += 8 * D
        wc = at(o, D, 8 * D).rearrange("p (b c) -> p b c", b=8); o += 8 * D
        w3l = hflat[:, 0:1024]
        idx_now = at(o, T, 4 * GS).bitcast(I32).rearrange("p (h s t) -> p h s t", h=2, s=2); o += 4 * GS
        zero16 = at(o, T, 256).bitcast(F16); o += 256
        iota3 = at(o, T, 1563).bitcast(U16)[:, 0:N]; o += 1563
        oh3 = at(o, T, 4 * 1563).bitcast(F16).rearrange("p (s n) -> p s n", s=4)[:, :, 0:N]; o += 4 * 1563
        vin = at(o, T, 4 * 256).bitcast(F16).rearrange("p (s q c) -> p s q c", s=4, q=4); o += 4 * 256
        msum = scratch[:, 0:N]
        assert o <= (NT * N + 3) // 2, o

        ld_edges, ld_x, ld_w0 = sem("ld_edges"), sem("ld_x"), sem("ld_w0")
        consts, iotas, eids, idx_float, lim_ready = sem("consts"), sem("iotas"), sem("eids"), sem("idx_float"), sem("lim_ready")
        ids_ps, lims_ps, ids_ready, range_cols, base_ps, tabc_ready, tab_ps, tab_ready = (
            sem("ids_ps"), sem("lims_ps"), sem("ids_ready"), sem("range_cols"), sem("base_ps"),
            sem("tabc_ready"), sem("tab_ps"), sem("tab_ready"))
        oh_ready, oh_used, ohd_built, last_chain = sem("oh_ready"), sem("oh_used"), sem("ohd_built"), sem("last_chain")
        adj_summed, last_turned, last_col = sem("adj_summed"), sem("last_turned"), sem("last_col")
        adj_by_act, adj_by_dve = sem("adj_by_act"), sem("adj_by_dve")
        chain = sem("dve_chain")
        x_ready, x_var, x_std = sem("x_ready"), sem("x_var"), sem("x_std")
        eidx_ready, ea_ready, eaug_ready = sem("eidx_ready"), sem("ea_ready"), sem("eaug_ready")
        sage = {k: sem(f"sage_{k}") for k in (
            "ft_ps", "ft_ready", "et_ps", "et_ready", "root_ps", "root_added", "tile_ready", "tile_used",
            "agg_out", "proj_ps", "proj_used", "ld")}
        gat = {k: sem(f"gat_{k}") for k in (
            "ld", "v_ready", "ft_ps", "ft_ready", "att_ps", "att_ready", "lim_cols", "lim_ps", "lim_rows", "lim_all",
            "seen_step", "seen_ps", "seen_turned", "seen_max", "cols_ready", "diag_ready", "row_ps", "row_ready",
            "shifted", "exped", "tile_ready", "tile_used", "agg_out", "proj_ps", "proj_used", "acc_step",
            "block_ready", "stored", "back", "w_zero")}
        bn = {k: sem(f"bn_{k}") for k in (
            "ld", "sum_ps", "sq_ready", "var_ps", "var_ready", "std_ready", "min_ready", "exp_ready", "hid_ready")}

        def sage_before(k):
            per = dict.fromkeys(sage, 1) | {
                "et_ps": NB, "et_ready": NB, "root_ps": NB, "root_added": NB, "tile_ready": NT * NB,
                "tile_used": NT * NB + SLOTS, "agg_out": NB, "proj_ps": NT, "proj_used": 3 * NT + 2, "ld": 0}
            return {name: k * count for name, count in per.items()}

        def gat_before(li):
            total = dict.fromkeys(gat, 0)
            for _, _, heads, _ in GAT[:li]:
                q = NB * heads
                per = dict.fromkeys(gat, 1) | {
                    "ld": 16 * 4, "att_ready": 0, "seen_step": heads * NT, "seen_turned": heads, "seen_max": heads,
                    "diag_ready": 2 * q, "row_ps": 2 * q, "row_ready": 2 * q, "shifted": q * NT, "exped": q * NT,
                    "tile_ready": q * NT, "tile_used": q * NT + SLOTS, "agg_out": q, "proj_ps": q * BT,
                    "proj_used": 2 * q * BT + 2, "acc_step": q + NB, "block_ready": NB, "stored": 16 * NB, "back": 16}
                total = {name: total[name] + per[name] for name in total}
            return total

        def bn_before(li):
            return {name: li * (32 if name == "ld" else 1) for name in bn}

        m3 = {k: sem(f"m3_{k}") for k in (
            "ld", "idx_ready", "w2T_ps", "w2T_ready", "wc_ps", "wc_ready", "ft_ps", "ft_ready", "p1_ps", "p1_ready", "qr_ps", "qr_ready",
            "stored", "hT_ps", "hT_ready", "g_ps", "prod_ready", "u_ready", "v_ready", "hi_ready",
            "lo_ready", "v_stored", "oh_ready", "oh_used", "sum_done", "sum_copied", "turned", "res_ready",
            "out_stored", "iota", "v_free", "sel_ready", "idx_now", "pool_turn")}
        gathered = [sem(f"gathered_{k}") for k in range(GS)]
        v_loaded = [sem(f"v_loaded_{k}") for k in range(4)]

        def bank_cols(j):
            return j // 4, (j % 4) * T

        def block_cols(i):
            return (0, i * T) if i < 3 else (1, (i - 3) * T)

        PIECES = ((0, 0, 3 * T), (1, 3 * T, 2 * T))

        block = ctx.enter_context(nc.Block())

        def tab_load(eng, which, w):
            return eng.value_load(table[0:1, ds(w + which * NT, 1)], min_val=0, max_val=NT * NG)

        @block.sync
        def _(sp):
            sp.dma_start(raw_src, p["src"].rearrange("(k q e) -> q k e", k=8, q=100)).then_inc(ld_edges, 16)
            sp.dma_start(raw_dst, p["dst"].rearrange("(k q e) -> q k e", k=8, q=100)).then_inc(ld_edges, 16)
            sp.dma_start(X[:, :, 0:D], p["x"].rearrange("(j q) c -> q j c", q=T)).then_inc(ld_x, 16)
            sp.dma_start(wbuf[0:D, 0:64], p["L0_gnn_W_l"]).then_inc(ld_w0, 16)
            sp.dma_start(wbuf[0:D, 64:128], p["L0_gnn_W_r"]).then_inc(ld_w0, 16)
            sp.dma_start(wbuf[0:16, 128:192], p["L0_gnn_W_e"]).then_inc(ld_w0, 16)
            sp.dma_start(wbuf[16:17, 128:192], p["L0_gnn_b_e"].rearrange("(a c) -> a c", a=1)).then_inc(ld_w0, 16)
            sp.dma_start(wbuf[0:1, 192:256], p["L0_gnn_b_l"].rearrange("(a c) -> a c", a=1)).then_inc(ld_w0, 16)
            for li, (n, fin, heads, fo) in enumerate(GAT):
                s, c = gat, gat_before(li)
                W, a_s, a_d, bias = (p[f"L1_gnn_{k}{li + 1}"] for k in ("W", "as", "ad", "b"))
                if li == 0:
                    sp.wait_ge(x_ready, 1)
                else:
                    sp.wait_ge(bn["hid_ready"], li)
                wn = heads * fo
                sp.dma_start(wbuf[0:fin, 0:wn], W).then_inc(s["ld"], 16)
                sp.dma_start(scratch[0:fin, 0:wn], a_s.rearrange("h c -> (h c)").partition_broadcast(fin)).then_inc(s["ld"], 16)
                sp.dma_start(scratch[0:fin, 512:512 + wn], a_d.rearrange("h c -> (h c)").partition_broadcast(fin)).then_inc(s["ld"], 16)
                sp.dma_start(wbuf[0:T, 512:512 + fo], bias.partition_broadcast(T)).then_inc(s["ld"], 16)
                gout = gat_out[n].rearrange("(j q) c -> q j c", q=T)
                with sp.Fori(0, NB) as b:
                    sp.wait_ge(s["block_ready"], c["block_ready"] + b + 1)
                    sp.dma_start(gout[:, ds(b * BT, BT), :], acc[:, :, 0:fo]).then_inc(s["stored"], 16)
                sp.wait_ge(s["stored"], c["stored"] + 16 * NB)
                if n == "c":
                    sp.dma_start(scratch[0:T, 0:NT * fo].rearrange("p (j c) -> p j c", j=NT), gout).then_inc(s["back"], 16)
                else:
                    sp.dma_start(hid, gout).then_inc(s["back"], 16)
                    for i, k in enumerate(("g", "be")):
                        sp.dma_start(rflat[0:T, i * 128:i * 128 + 128],
                                     p[f"L1_gnn_{k}{li + 1}"].partition_broadcast(T)).then_inc(bn["ld"], 16)
            sp.wait_ge(x_ready, 2)
            s, c = sage, sage_before(1)
            sp.dma_start(wbuf[0:D, 0:64], p["L2_gnn_W"][D:2 * D, :]).then_inc(s["ld"], 16)
            sp.dma_start(wbuf[0:D, 64:128], p["L2_gnn_W"][0:D, :]).then_inc(s["ld"], 16)
            sp.dma_start(wbuf[0:1, 192:256], p["L2_gnn_b"].rearrange("(a c) -> a c", a=1)).then_inc(s["ld"], 16)
            s = m3
            sp.wait_ge(x_ready, 3)
            sp.dma_start(idx3[:, 0, :], p["src"].rearrange("(q t) -> q t", q=T)).then_inc(s["ld"], 16)
            sp.dma_start(idx3[:, 1, :], p["dst"].rearrange("(q t) -> q t", q=T)).then_inc(s["ld"], 16)
            sp.dma_start(basis, p["edge_attr_8"].rearrange("(q t) b -> q t b", q=T)).then_inc(s["ld"], 16)
            sp.dma_start(w3l[0:D, 0:64], p["L3_gnn_pp_W"]).then_inc(s["ld"], 16)
            sp.dma_start(w3l[0:D, 64:128], p["L3_gnn_pi_W1"][0:D, :]).then_inc(s["ld"], 16)
            sp.dma_start(w3l[0:D, 128:192], p["L3_gnn_pi_W1"][D:2 * D, :]).then_inc(s["ld"], 16)
            sp.dma_start(w3l[0:D, 192:256], p["L3_gnn_ii_W"]).then_inc(s["ld"], 16)
            sp.dma_start(w3l[0:D, 256:768], p["L3_gnn_pi_W2"]).then_inc(s["ld"], 16)
            sp.dma_start(w3l[0:D, 768:769], p["L3_gnn_pp_b"].rearrange("(c a) -> c a", a=1)).then_inc(s["ld"], 16)
            sp.dma_start(w3l[0:1, 896:960], p["L3_gnn_pi_b1"].rearrange("(a c) -> a c", a=1)).then_inc(s["ld"], 16)
            for k in range(2):
                sp.dma_start(prod[:, k, 8, :], p["L3_gnn_ii_b"].partition_broadcast(T)).then_inc(s["ld"], 16)
            sp.sem_inc(s["v_free"], 2)
            sp.wait_ge(s["qr_ready"], 1)
            sp.dma_start(q_dram.rearrange("(j q) c -> q j c", q=T), qr[:, :, 0:D]).then_inc(s["stored"], 16)
            sp.dma_start(r_dram.rearrange("(j q) c -> q j c", q=T), qr[:, :, D:2 * D]).then_inc(s["stored"], 16)
            with sp.Fori(0, NCH // 8) as i:
                for k in range(2):
                    sp.wait_ge(s["lo_ready"], 2 * i + k + 3)
                    sp.dma_start(v_dram[ds(2 * i + k, 1), :, :].rearrange("a q c -> q (a c)"),
                                 vsplit[:, k].rearrange("p q h c -> p (q h c)")).then_inc(s["v_stored"], 16)
                    sp.wait_ge(s["v_stored"], 16 * (2 * i + k) + 16)
                    sp.sem_inc(s["v_free"], 1)
            with sp.Fori(0, NCH // 16) as i:
                for k in range(4):
                    sp.wait_ge(s["oh_used"], 4 * (4 * i + k) + 4)
                    sp.dma_start(vin[:, k], v_dram[ds(4 * i + k, 1), :, :].rearrange("a q (g c) -> q (a g) c", g=4)).then_inc(v_loaded[k], 16)
            sp.wait_ge(x_ready, 4)
            sp.dma_start(out.rearrange("(j q) c -> q j c", q=T), X[:, :, 0:D]).then_inc(s["out_stored"], 16)
            sp.wait_ge(s["out_stored"], 16)

        @block.gpsimd
        def _(pool):
            g = nc.gpsimd
            g.memset(ident[:], 0.0).then_inc(consts, 1)
            g.memset(ones[:], 1.0).then_inc(consts, 1)
            g.memset(lower, 1.0).then_inc(consts, 1)
            g.memset(X[:, :, D:D + 1], 1.0).then_inc(consts, 1)
            pool.wait_ge(consts, 4)
            g.affine_select(out=ident[:], in_=ident[:], compare_op=ALU.not_equal, fill=1.0, base=0,
                            pattern=[[-1, 128]], channel_multiplier=1).then_inc(consts, 1)
            g.affine_select(out=lower, in_=lower, compare_op=ALU.is_gt, fill=0.0, base=0,
                            pattern=[[1, NT]], channel_multiplier=-1).then_inc(consts, 1)
            g.iota(fwd, [[1, NG]], base=1, channel_multiplier=0, allow_small_or_imprecise_dtypes=True).then_inc(consts, 1)
            g.iota(rev, [[-1, NG]], base=NG, channel_multiplier=0, allow_small_or_imprecise_dtypes=True).then_inc(consts, 1)
            g.iota(wcol[:, 0:1], [[0, 1]], base=0, channel_multiplier=T, allow_small_or_imprecise_dtypes=True).then_inc(consts, 1)
            pool.wait_ge(idx_float, 2)
            g.iota(eid, [[T, NCH]], base=1, channel_multiplier=1, allow_small_or_imprecise_dtypes=True).then_inc(eids, 1)
            pool.wait_ge(tab_ready, 1)
            g.iota(iota, [[1, N]], base=0, channel_multiplier=0).then_inc(iotas, 1)
            g.memset(zeros, 0.0).then_inc(iotas, 1)
            pool.wait_ge(eidx_ready, 1)
            for j in range(NT):
                g.indirect_dma_start(ea[:, j, :], None, p["edge_attr_16"],
                                     bass.IndirectOffsetOnAxis(ap=eidx[:, j:j + 1], axis=0)).then_inc(ea_ready, 16)
            s = m3
            pool.wait_ge(x_ready, 3)
            g.iota(iota3, [[1, N]], base=0, channel_multiplier=0).then_inc(s["iota"], 1)
            g.memset(zero16, 0.0).then_inc(s["iota"], 1)
            pool.wait_ge(s["stored"], 32)
            pool.wait_ge(s["ld"], 16 * 12)
            with pool.Fori(0, NCH // (2 * GS)) as i:
                for half in range(2):
                    t0 = (2 * i + half) * GS
                    pool.wait_ge(s["hT_ps"], t0)
                    pool.sem_inc(s["pool_turn"], 1)
                    g.tensor_copy(idx_now[:, half], idx3[:, :, ds(t0, GS)]).then_inc(s["idx_now"], 1)
                    pool.wait_ge(s["idx_now"], 2 * i + half + 1)
                    pool.sem_inc(s["pool_turn"], 1)
                    for k in range(GS):
                        pool.wait_ge(s["hT_ps"], t0 + k + 1)
                        pool.sem_inc(s["pool_turn"], 1)
                        for a, table_dram in enumerate((q_dram, r_dram)):
                            g.indirect_dma_start(gath[:, k, a, :], None, table_dram,
                                                 bass.IndirectOffsetOnAxis(ap=idx_now[:, half, a, k:k + 1], axis=0)).then_inc(gathered[k], 16)

        @block.scalar
        def _(act):
            a = nc.scalar
            with act.Fori(0, NT) as w:
                act.wait_ge(adj_summed, w + 1)
                a.copy(adj3[:, 0:16, ds(w * T, T)].rearrange("p (b j) d -> p b j d", b=4),
                       ps[0:T, 0:4, 0:500].rearrange("p b (j d) -> p b j d", j=4)).then_inc(adj_by_act, 1)

            def copy_ft(s, fin, done):
                act.wait_ge(s["ft_ps"], done + 1)
                a.copy(ft[0:fin, 0:3000].rearrange("p (b d) -> p b d", b=6), ps[0:fin, 0:6, 0:500])
                a.copy(ft[0:fin, 3000:N], ps[0:fin, 6, 0:T]).then_inc(s["ft_ready"], 1)

            def layernorm_std(k):
                act.wait_ge(x_var, k)
                a.activation(rflat[0:T, 50:75], rflat[0:T, 25:50], ACT.Sqrt).then_inc(x_std, 1)

            def sage_layer(k):
                s, c = sage, sage_before(k)
                copy_ft(s, D, k)
                if k == 0:
                    for b in range(NB):
                        act.wait_ge(s["et_ps"], c["et_ps"] + b + 1)
                        for bank, c0, n in PIECES:
                            i = a.copy(aggT[0:17, c0:c0 + n], ps[0:17, bank, 0:n])
                        i.then_inc(s["et_ready"], 1)
                act.wait_ge(s["root_ps"], c["root_ps"] + NB)
                with act.Fori(0, NB) as b:
                    for j in range(NT):
                        act.wait_ge(s["tile_used"], c["tile_used"] + b * NT + j + 1)
                        a.copy(slots[:, j % SLOTS, :], adj3[:, j, ds(b * BW, BW)]).then_inc(s["tile_ready"], 1)
                    act.wait_ge(s["tile_used"], c["tile_used"] + b * NT + NT + SLOTS)
                    act.wait_ge(s["proj_ps"], c["proj_ps"] + b * BT)
                    for bank, c0, n in PIECES:
                        i = a.copy(aggT[0:D + 1, c0:c0 + n], ps[0:D + 1, bank, 0:n])
                    i.then_inc(s["agg_out"], 1)

            sage_layer(0)
            layernorm_std(1)
            for li, (n, fin, heads, fo) in enumerate(GAT):
                s, c = gat, gat_before(li)
                act.wait_ge(s["v_ready"], c["v_ready"] + 1)
                copy_ft(s, fin, li)
                if n == "c":
                    act.wait_ge(s["att_ps"], c["att_ps"] + 1)
                    a.copy(h3[:, 0:24, 0:D].rearrange("p (b j) c -> p b j c", b=3),
                           ps[0:T, 0:3, :].rearrange("p b (j c) -> p b j c", j=8))
                    a.copy(h3[:, 24, 0:D], ps[0:T, 3, 0:D]).then_inc(s["att_ready"], 1)
                with act.Fori(0, NB) as b:
                    with act.Fori(0, heads) as h:
                        q = b * heads + h
                        for r in range(2):
                            act.wait_ge(s["row_ps"], c["row_ps"] + 2 * q + r + 1)
                            if r == 0:
                                act.wait_ge(s["shifted"], c["shifted"] + q * NT)
                            for bank, c0, nn in PIECES:
                                i = a.copy(rows[0:T, r, c0:c0 + nn], ps[0:T, 4 + bank, 0:nn])
                            i.then_inc(s["row_ready"], 1)
                        for j in range(NT):
                            act.wait_ge(s["shifted"], c["shifted"] + q * NT + j + 1)
                            a.activation(slots[:, j % SLOTS, :], slots[:, j % SLOTS, :], ACT.Exp,
                                         bias=cols[:, 4, j, ds(h, 1)]).then_inc(s["exped"], 1)
                        act.wait_ge(s["tile_used"], c["tile_used"] + q * NT + NT + SLOTS)
                        act.wait_ge(s["proj_ps"], c["proj_ps"] + q * BT)
                        for bank, c0, nn in PIECES:
                            m = 128 if n == "b" else D + 1
                            i = a.copy(aggT[0:m, c0:c0 + nn], ps[0:m, bank, 0:nn])
                            if n == "b":
                                i = a.copy(dent[0:1, c0:c0 + nn], ps[0:1, 2 + bank, 0:nn])
                        i.then_inc(s["agg_out"], 1)
                if n != "c":
                    t, tc = bn, bn_before(li)
                    act.wait_ge(t["var_ready"], tc["var_ready"] + 1)
                    a.activation(rflat[0:T, 512:640], rflat[0:T, 384:512], ACT.Sqrt).then_inc(t["std_ready"], 1)
                    act.wait_ge(t["min_ready"], tc["min_ready"] + 1)
                    a.activation(scratch[0:T, 0:3200], scratch[0:T, 0:3200], ACT.Exp).then_inc(t["exp_ready"], 1)
            layernorm_std(2)
            sage_layer(1)
            layernorm_std(3)
            s = m3
            copy_ft(s, D, 0)
            act.wait_ge(s["w2T_ps"], 1)
            a.copy(w2T, ps[0:D, 7, :].rearrange("p (b k) -> p b k", b=8)).then_inc(s["w2T_ready"], 1)
            act.wait_ge(s["wc_ps"], 1)
            a.copy(wc, ps[0:D, 7, :].rearrange("p (b c) -> p b c", b=8)).then_inc(s["wc_ready"], 1)
            act.wait_ge(s["p1_ps"], 1)
            for b in range(BANKS):
                nn = 500 if b < 6 else T
                i = a.activation(p1T[:, b * 500:b * 500 + nn], ps[0:D, b, 0:nn], ACT.Tanh, bias=w3l[0:D, 768:769])
            i.then_inc(s["p1_ready"], 1)
            act.wait_ge(s["qr_ps"], 1)
            a.copy(qr[:, 0:24, :].rearrange("p (b j) c -> p b j c", b=6), ps[0:T, 0:6, :].rearrange("p b (j c) -> p b j c", j=4))
            a.copy(qr[:, 24, :], ps[0:T, 6, 0:128]).then_inc(s["qr_ready"], 1)
            act.sem_inc(s["v_ready"], 2)
            with act.Fori(0, NCH // 8) as i8:
                for k in range(8):
                    t = 8 * i8 + k
                    act.wait_ge(s["hT_ps"], t + 1 + GS)
                    act.wait_ge(s["g_ps"], t + 1)
                    a.copy(hT[:, k % 4, :], ps[0:D, k % 2, 0:T]).then_inc(s["hT_ready"], 1)
                    if k % 4 == 3:
                        z = 2 * i8 + k // 4
                        act.wait_ge(s["u_ready"], t + 1)
                        act.wait_ge(s["lo_ready"], z + 1)
                        a.activation(vval[:, k // 4], uval[:, k // 4], ACT.Tanh).then_inc(s["v_ready"], 1)
                        act.wait_ge(s["v_ready"], z + 3)
                        act.wait_ge(s["v_free"], z + 1)
                        a.copy(vsplit[:, k // 4, :, 0, :], vval[:, k // 4]).then_inc(s["hi_ready"], 1)
            act.wait_ge(s["sum_done"], 1)
            a.copy(msum[:, 0:3000].rearrange("p (b d) -> p b d", b=6), ps[:, 0:6, 0:500])
            a.copy(msum[:, 3000:N], ps[:, 6, 0:T]).then_inc(s["sum_copied"], 1)
            layernorm_std(4)

        @block.vector
        def _(dve):
            v = nc.vector
            links = [0]

            def link(ins):
                links[0] += 1
                ins.then_inc(chain, 1)
                dve.wait_ge(chain, links[0])

            dve.wait_ge(ld_edges, 32)
            v.tensor_copy(flt_src, raw_src).then_inc(idx_float, 1)
            v.tensor_copy(flt_dst, raw_dst).then_inc(idx_float, 1)
            dve.wait_ge(idx_float, 2)
            v.tensor_reduce(chunk_lim[:, 0, :], flt_dst, X_AXIS, ALU.max)
            v.tensor_reduce(chunk_lim[:, 1, :], flt_dst, X_AXIS, ALU.min).then_inc(lim_ready, 1)
            dve.wait_ge(ids_ps, 1)
            v.tensor_copy(edge_ids[:].rearrange("p s (b c) -> p (s b) c", b=2), ps[0:T, 0:4, 0:400]).then_inc(ids_ready, 1)
            dve.wait_ge(lims_ps, 1)
            dve.wait_ge(consts, 9)
            for b in range(2):
                v.tensor_reduce(gmax[:, b * 200:b * 200 + 200], ps[0:NT, 4 + b, 0:400].rearrange("p (g c) -> p g c", c=2), X_AXIS, ALU.max)
                i = v.tensor_reduce(gmin[:, b * 200:b * 200 + 200], ps[0:NT, 6 + b, 0:400].rearrange("p (g c) -> p g c", c=2), X_AXIS, ALU.min)
            link(i)
            link(v.tensor_scalar(wcol[:, 1:2], wcol[:, 0:1], float(T - 1), None, ALU.add))
            link(v.scalar_tensor_tensor(tmpg, gmax, wcol[:, 0:1], rev, ALU.is_ge, ALU.mult))
            link(v.tensor_reduce(wcol[:, 2:3], tmpg, X_AXIS, ALU.max))
            link(v.tensor_scalar(wcol[:, 3:4], wcol[:, 2:3], -1.0, float(NG), ALU.mult, ALU.add))
            link(v.tensor_scalar(wcol[:, 3:4], wcol[:, 3:4], float(NG - 1), None, ALU.min))
            link(v.scalar_tensor_tensor(tmpg, gmin, wcol[:, 1:2], fwd, ALU.is_le, ALU.mult))
            link(v.tensor_reduce(wcol[:, 4:5], tmpg, X_AXIS, ALU.max))
            link(v.tensor_tensor(wcol[:, 5:6], wcol[:, 4:5], wcol[:, 3:4], ALU.subtract))
            link(v.tensor_scalar(wcol[:, 5:6], wcol[:, 5:6], 1.0, None, ALU.max))
            v.nop().then_inc(range_cols, 1)
            dve.wait_ge(base_ps, 1)
            link(v.tensor_copy(wcol[:, 6:7], ps[0:NT, 0, 0:1]))
            link(v.tensor_tensor(wcol[:, 7:8], wcol[:, 6:7], wcol[:, 5:6], ALU.add))
            link(v.tensor_tensor(wcol[:, 8:9], wcol[:, 6:7], wcol[:, 3:4], ALU.subtract))
            v.nop().then_inc(tabc_ready, 1)
            dve.wait_ge(tab_ps, 1)
            v.tensor_copy(table[:], ps[0:1, 1, 0:3 * NT]).then_inc(tab_ready, 1)
            dve.wait_ge(tab_ready, 1)
            dve.wait_ge(iotas, 2)
            dve.wait_ge(eids, 1)
            dve.wait_ge(ids_ready, 1)
            dve.sem_inc(oh_used, PAIR)
            with dve.Fori(0, NT) as w:
                k0, k1, back = (tab_load(dve, i, w) for i in range(3))
                dve.wait_ge(last_turned, w)
                v.memset(lastmax, 0.0).then_inc(last_chain, 1)
                with dve.Fori(k0, k1) as k:
                    g = dve.snap(nc.s_assert_within(k - back, 0, NG - 1, skip_runtime_bounds_check_because="a window's steps lie in 0 to NG"))
                    for c in range(PAIR):
                        dve.wait_ge(oh_used, k * PAIR + c + 1)
                        v.tensor_scalar(onehot_dst[:, c, :], iota[:, ds(w * T, T)], edge_ids[:, 1, ds(g * PAIR + c, 1)],
                                        None, ALU.is_equal).then_inc(ohd_built, 1)
                        v.tensor_scalar(onehot_src[:, c, :], iota, edge_ids[:, 0, ds(g * PAIR + c, 1)],
                                        None, ALU.is_equal).then_inc(oh_ready, 1)
                        dve.wait_ge(ohd_built, k * PAIR + c + 1)
                        dve.wait_ge(last_chain, k * PAIR + w + c + 1)
                        v.scalar_tensor_tensor(lastmax, onehot_dst[:, c, :], eid[:, ds(g * PAIR + c, 1)], lastmax,
                                               ALU.mult, ALU.max).then_inc(last_chain, 1)
                dve.wait_ge(adj_summed, w + 1)
                v.tensor_copy(adj3[:, 16:24, ds(w * T, T)].rearrange("p (b j) d -> p b j d", b=2),
                              ps[0:T, 4:6, 0:500].rearrange("p b (j d) -> p b j d", j=4))
                v.tensor_copy(adj3[:, 24, ds(w * T, T)], ps[0:T, 6, 0:T]).then_inc(adj_by_dve, 1)
                dve.wait_ge(last_turned, w + 1)
                v.tensor_reduce(last_edge[:, ds(w, 1)], ps[0:T, 7, 0:T], X_AXIS, ALU.max).then_inc(last_col, 1)
            dve.wait_ge(last_col, NT)
            link(v.tensor_scalar(small[0:T, 0:NT], last_edge[:], -1.0, 0.0, ALU.add, ALU.max))
            v.tensor_copy(eidx, small[0:T, 0:NT]).then_inc(eidx_ready, 1)
            link(v.tensor_scalar(small[0:T, NT:2 * NT], last_edge[:], 1.0, None, ALU.min))
            has = small[0:T, NT:2 * NT].unsqueeze(2)
            dve.wait_ge(ea_ready, 16 * NT)
            v.tensor_copy(eaug[:, :, 16:17], has)
            v.tensor_tensor(eaug[:, :, 0:16], ea, has.to_broadcast([T, NT, 16]), ALU.mult).then_inc(eaug_ready, 1)

            def sage_layer(k):
                s, c = sage, sage_before(k)
                for b in range(NB):
                    dve.wait_ge(s["root_ps"], c["root_ps"] + b + 1)
                    v.tensor_tensor(res[:, b * BT:b * BT + BT, :], ps[0:T, 2, 0:BT * D].rearrange("p (i c) -> p i c", i=BT),
                                    X[:, b * BT:b * BT + BT, 0:D], ALU.add).then_inc(s["root_added"], 1)
                dve.wait_ge(s["root_added"], c["root_added"] + NB)
                with dve.Fori(0, NB) as b:
                    for i in range(BT):
                        dve.wait_ge(s["proj_ps"], c["proj_ps"] + b * BT + i + 1)
                        pr = ps[0:T, 6 + i % 2, :]
                        deg = small[0:T, 2 * i:2 * i + 2]
                        v.tensor_scalar(deg[:, 0:1], pr[:, 128:129], 1.0, None, ALU.max).then_inc(s["proj_used"], 1)
                        dve.wait_ge(s["proj_used"], c["proj_used"] + 3 * (b * BT + i) + 2 + 1)
                        v.reciprocal(deg[:, 1:2], deg[:, 0:1]).then_inc(s["proj_used"], 1)
                        dve.wait_ge(s["proj_used"], c["proj_used"] + 3 * (b * BT + i) + 2 + 2)
                        tile = res[:, ds(b * BT + i, 1), :].rearrange("p a c -> p (a c)")
                        v.scalar_tensor_tensor(tile, pr[:, 0:D], deg[:, 1:2], tile, ALU.mult, ALU.add).then_inc(s["proj_used"], 1)
                dve.wait_ge(s["proj_used"], c["proj_used"] + 3 * NT + 2)

            def layernorm(k):
                mean, var, std = (rflat[0:T, i:i + NT] for i in (0, 25, 50))
                link(v.tensor_reduce(mean, res, X_AXIS, ALU.add))
                link(v.tensor_scalar(mean, mean, 1.0 / D, None, ALU.mult))
                link(v.tensor_tensor(res, res, mean.unsqueeze(2).to_broadcast([T, NT, D]), ALU.subtract))
                sq = scratch[0:T, 0:NT * D].rearrange("p (j c) -> p j c", j=NT)
                link(v.tensor_tensor(sq, res, res, ALU.mult))
                link(v.tensor_reduce(var, sq, X_AXIS, ALU.add))
                link(v.tensor_scalar(var, var, 1.0 / D, EPS, ALU.mult, ALU.add))
                v.nop().then_inc(x_var, 1)
                dve.wait_ge(x_std, k)
                link(v.reciprocal(std, std))
                link(v.tensor_tensor(X[:, :, 0:D], res, std.unsqueeze(2).to_broadcast([T, NT, D]), ALU.mult))

            def self_loops(op):
                for j in range(NT):
                    d = adj3[:, j, j * T:j * T + T]
                    i = v.tensor_tensor(d, d, ident[0:T, 0:T], op)
                link(i)

            dve.sem_inc(sage["proj_used"], 2)
            sage_layer(0)
            layernorm(1)
            v.nop().then_inc(x_ready, 1)
            self_loops(ALU.add)
            for li, (n, fin, heads, fo) in enumerate(GAT):
                s, c = gat, gat_before(li)
                wn = heads * fo
                if n == "a":
                    v.memset(wbuf[D:D + 1, 0:wn], 0.0).then_inc(s["w_zero"], 1)
                dve.wait_ge(s["ld"], c["ld"] + 16 * 4)
                for i in range(2):
                    prodw = scratch[0:fin, 1024:1024 + wn]
                    link(v.tensor_tensor(prodw, wbuf[0:fin, 0:wn], scratch[0:fin, 512 * i:512 * i + wn], ALU.mult))
                    link(v.tensor_reduce(small[0:fin, i * heads:(i + 1) * heads], prodw.rearrange("p (h c) -> p h c", h=heads), X_AXIS, ALU.add))
                v.nop().then_inc(s["v_ready"], 1)
                H2 = 2 * heads
                dve.wait_ge(s["att_ps"], c["att_ps"] + 1)
                link(v.tensor_copy(att[:, :, 0:H2], ps[0:T, 7, 0:NT * H2].rearrange("p (j h) -> p j h", j=NT)))
                a_src, a_dst = att[:, :, 0:heads], att[:, :, heads:H2]
                if n == "c":
                    v.memset(h3[:, :, D:D + 1], 1.0).then_inc(s["att_ready"], 1)
                link(v.tensor_reduce(small[0:T, 8:8 + heads], a_src.rearrange("p j h -> p h j"), X_AXIS, ALU.max))
                link(v.tensor_reduce(small[0:T, 8 + heads:8 + H2], a_src.rearrange("p j h -> p h j"), X_AXIS, ALU.min))
                link(v.tensor_scalar(small[0:T, 8 + heads:8 + H2], small[0:T, 8 + heads:8 + H2], -1.0, None, ALU.mult))
                v.nop().then_inc(s["lim_cols"], 1)
                dve.wait_ge(s["lim_ps"], c["lim_ps"] + 1)
                link(v.tensor_reduce(small[0:H2, 16:17], ps[0:H2, 6, 0:T], X_AXIS, ALU.max))
                v.nop().then_inc(s["lim_rows"], 1)
                dve.wait_ge(s["lim_all"], c["lim_all"] + 1)
                link(v.tensor_copy(small[0:T, 20:20 + H2], ps[0:T, 5, 0:H2]))
                top, nbot = small[0:T, 20:20 + heads], small[0:T, 20 + heads:20 + H2]
                rng, inv = small[0:T, 28:28 + heads], small[0:T, 32:32 + heads]
                link(v.tensor_tensor(rng, top, nbot, ALU.add))
                link(v.tensor_scalar(inv, rng, 1e-30, None, ALU.max))
                link(v.reciprocal(inv, inv))

                def by_head(c):
                    return c.unsqueeze(1).to_broadcast([T, NT, heads])

                A, asn, r1, r2, s02, s08 = (cols[:, i, :, 0:heads] for i in range(6))
                link(v.tensor_tensor(asn, a_src, by_head(nbot), ALU.add))
                link(v.tensor_tensor(asn, asn, by_head(inv), ALU.mult))
                link(v.tensor_scalar(asn, asn, 1.0, None, ALU.min))
                dve.wait_ge(s["att_ps"], c["att_ps"] + 1)
                with dve.Fori(0, heads) as h:
                    dve.wait_ge(s["seen_turned"], c["seen_turned"] + h)
                    v.tensor_scalar(seen, adj3[:, 0, :], asn[:, 0, ds(h, 1)], None, ALU.min).then_inc(s["seen_step"], 1)
                    for j in range(1, NT):
                        dve.wait_ge(s["seen_step"], c["seen_step"] + h * NT + j)
                        v.scalar_tensor_tensor(seen, adj3[:, j, :], asn[:, j, ds(h, 1)], seen, ALU.min, ALU.max).then_inc(s["seen_step"], 1)
                    dve.wait_ge(s["seen_turned"], c["seen_turned"] + h + 1)
                    v.tensor_reduce(A[:, 0:24, ds(h, 1)].rearrange("p (b j) h -> p b (j h)", b=6),
                                    ps[0:T, 0:6, 0:500].rearrange("p b (j e) -> p b j e", j=4), X_AXIS, ALU.max)
                    v.tensor_reduce(A[:, 24, ds(h, 1)], ps[0:T, 6, 0:T], X_AXIS, ALU.max).then_inc(s["seen_max"], 1)
                dve.wait_ge(s["seen_max"], c["seen_max"] + heads)
                link(v.tensor_tensor(A, A, by_head(rng), ALU.mult))
                link(v.tensor_tensor(A, A, by_head(nbot), ALU.subtract))
                link(v.tensor_tensor(A, A, a_dst, ALU.add))
                link(v.scalar_tensor_tensor(A, A, NEG, A, ALU.mult, ALU.max))
                link(v.tensor_tensor(r1, a_dst, A, ALU.subtract))
                link(v.scalar_tensor_tensor(r2, a_dst, NEG, A, ALU.mult, ALU.subtract))
                link(v.tensor_scalar(s02, a_src, NEG, None, ALU.mult))
                link(v.tensor_scalar(s08, a_src, 1.0 - NEG, None, ALU.mult))
                v.nop().then_inc(s["cols_ready"], 1)
                dve.sem_inc(s["tile_used"], SLOTS)
                dve.sem_inc(s["proj_used"], 2)
                with dve.Fori(0, NB) as b:
                    dve.wait_ge(s["stored"], c["stored"] + b * 16)
                    v.memset(acc[:], 0.0).then_inc(s["acc_step"], 1)
                    with dve.Fori(0, heads) as h:
                        q = b * heads + h
                        for r, col in enumerate((r1, r2)):
                            dve.wait_ge(s["row_ps"], c["row_ps"] + 2 * q + r)
                            v.tensor_tensor(diag, ident[0:T, 0:T].unsqueeze(1).to_broadcast([T, BT, T]),
                                            col[:, ds(b * BT, BT), ds(h, 1)].to_broadcast([T, BT, T]), ALU.mult).then_inc(s["diag_ready"], 1)
                        dve.wait_ge(s["row_ready"], c["row_ready"] + 2 * q + 2)
                        for j in range(NT + 2):
                            if j < NT:
                                dve.wait_ge(s["tile_used"], c["tile_used"] + q * NT + j + 1)
                                v.scalar_tensor_tensor(slots[:, j % SLOTS, :], rows[0:T, 0, :], s08[:, j, ds(h, 1)], rows[0:T, 1, :],
                                                       ALU.add, ALU.max).then_inc(s["shifted"], 1)
                            if j >= 2:
                                m = j - 2
                                dve.wait_ge(s["exped"], c["exped"] + q * NT + m + 1)
                                v.tensor_tensor(slots[:, m % SLOTS, :], slots[:, m % SLOTS, :], adj3[:, m, ds(b * BW, BW)],
                                                ALU.mult).then_inc(s["tile_ready"], 1)
                        for i in range(BT):
                            dve.wait_ge(s["proj_ps"], c["proj_ps"] + q * BT + i + 1)
                            pr = ps[0:T, 6 + i % 2, :]
                            inv_den = small[0:T, 40 + i:41 + i]
                            v.reciprocal(inv_den, pr[:, 128:129]).then_inc(s["proj_used"], 1)
                            dve.wait_ge(s["proj_used"], c["proj_used"] + 2 * (q * BT + i) + 2 + 1)
                            dve.wait_ge(s["acc_step"], c["acc_step"] + b + 1 + q)
                            v.scalar_tensor_tensor(acc[:, i, 0:fo], pr[:, 0:fo], inv_den, acc[:, i, 0:fo], ALU.mult, ALU.add).then_inc(s["proj_used"], 1)
                        dve.wait_ge(s["proj_used"], c["proj_used"] + 2 * (q * BT + BT) + 2)
                        v.nop().then_inc(s["acc_step"], 1)
                    v.scalar_tensor_tensor(acc[:, :, 0:fo], acc[:, :, 0:fo], 1.0 / heads,
                                           wbuf[0:T, 512:512 + fo].unsqueeze(1).to_broadcast([T, BT, fo]),
                                           ALU.mult, ALU.add).then_inc(s["block_ready"], 1)
                dve.wait_ge(s["back"], c["back"] + 16)
                if n != "c":
                    t, tc = bn, bn_before(li)
                    gam, bet, mu, var, std = (rflat[0:T, i * 128:i * 128 + 128] for i in range(5))
                    dve.wait_ge(t["ld"], tc["ld"] + 32)

                    def row(c):
                        return c.unsqueeze(1).to_broadcast([T, NT, 128])

                    dve.wait_ge(t["sum_ps"], tc["sum_ps"] + 1)
                    link(v.tensor_scalar(mu, ps[0:T, 0, 0:128], 1.0 / N, None, ALU.mult))
                    link(v.tensor_tensor(hid, hid, row(mu), ALU.subtract))
                    sq = scratch[0:T, 0:3200].rearrange("p (j c) -> p j c", j=NT)
                    v.tensor_tensor(sq, hid, hid, ALU.mult).then_inc(t["sq_ready"], 1)
                    dve.wait_ge(t["var_ps"], tc["var_ps"] + 1)
                    v.tensor_scalar(var, ps[0:T, 1, 0:128], 1.0 / N, EPS, ALU.mult, ALU.add).then_inc(t["var_ready"], 1)
                    dve.wait_ge(t["std_ready"], tc["std_ready"] + 1)
                    link(v.reciprocal(std, std))
                    link(v.tensor_tensor(std, std, gam, ALU.mult))
                    link(v.tensor_tensor(hid, hid, row(std), ALU.mult))
                    link(v.tensor_tensor(hid, hid, row(bet), ALU.add))
                    v.tensor_scalar(sq, hid, 0.0, None, ALU.min).then_inc(t["min_ready"], 1)
                    dve.wait_ge(t["exp_ready"], tc["exp_ready"] + 1)
                    link(v.tensor_scalar(sq, sq, -1.0, None, ALU.add))
                    v.scalar_tensor_tensor(hid, hid, 0.0, sq, ALU.max, ALU.add).then_inc(t["hid_ready"], 1)
                    dve.wait_ge(t["hid_ready"], tc["hid_ready"] + 1)
            g3 = scratch[0:T, 0:NT * D].rearrange("p (j c) -> p j c", j=NT)
            link(v.tensor_tensor(res, g3, X[:, :, 0:D], ALU.add))
            layernorm(2)
            v.nop().then_inc(x_ready, 1)
            self_loops(ALU.subtract)
            dve.sem_inc(sage["proj_used"], 2)
            sage_layer(1)
            layernorm(3)
            v.nop().then_inc(x_ready, 1)
            s = m3
            dve.wait_ge(s["ld"], 16 * 12)
            v.tensor_copy(src3, idx3[:, 0, :]).then_inc(s["idx_ready"], 1)
            link(v.tensor_tensor(small[:, 0:D], ident[:, 0:D], ident[:, D:2 * D], ALU.add))
            v.nop().then_inc(s["sel_ready"], 1)
            dve.sem_inc(s["g_ps"], 4)
            dve.sem_inc(s["prod_ready"], 1)
            dve.sem_inc(s["lo_ready"], 2)
            with dve.Fori(0, NCH // 8) as i8:
                for k in range(8):
                    t = 8 * i8 + k
                    dve.wait_ge(s["g_ps"], t + 1 + 4)
                    v.tensor_tensor(prod[:, k % 2, 0:8, :], ps[0:T, 2 + k % 2, :].rearrange("p (b c) -> p b c", b=8),
                                    basis[:, ds(t, 1), :].rearrange("p a b -> p (a b)").unsqueeze(2).to_broadcast([T, 8, D]),
                                    ALU.mult).then_inc(s["prod_ready"], 1)
                    dve.wait_ge(s["prod_ready"], t + 2)
                    if k % 4 == 0:
                        dve.wait_ge(s["v_ready"], 2 * i8 + k // 4 + 1)
                    v.tensor_reduce(uval[:, k // 4, k % 4, :], prod[:, k % 2].rearrange("p b c -> p c b"), X_AXIS, ALU.add).then_inc(s["u_ready"], 1)
                    if k % 4 == 3:
                        z = 2 * i8 + k // 4
                        dve.wait_ge(s["hi_ready"], z + 1)
                        v.tensor_tensor(vsplit[:, k // 4, :, 1, :], vval[:, k // 4], vsplit[:, k // 4, :, 0, :], ALU.subtract).then_inc(s["lo_ready"], 1)
            dve.wait_ge(s["idx_ready"], 1)
            dve.wait_ge(s["iota"], 1)
            with dve.Fori(0, NCH // 4) as i4:
                for k in range(4):
                    dve.wait_ge(s["oh_used"], 4 * i4 + k + 13)
                    v.tensor_scalar(oh3[:, k, :], iota3, src3[:, ds(4 * i4 + k, 1)], None, ALU.is_equal).then_inc(s["oh_ready"], 1)
            dve.wait_ge(s["turned"], 1)
            for b in range(4):
                n8 = 8 if b < 3 else 1
                i = v.scalar_tensor_tensor(res[:, b * 8:b * 8 + n8, :], X[:, b * 8:b * 8 + n8, 0:D], 2.0,
                                           ps[0:T, b, 0:n8 * D].rearrange("p (j c) -> p j c", j=n8), ALU.mult, ALU.add)
            link(i)
            layernorm(4)
            v.nop().then_inc(x_ready, 1)

        @block.tensor
        def _(pe):
            t_ = nc.tensor

            def mm(o_, l, r, start=True, stop=True, skip=False):
                return t_.matmul(o_, l, r, start=start, stop=stop, skip_group_check=skip)

            I = ident
            pe.wait_ge(idx_float, 2)
            pe.wait_ge(consts, 9)
            for s_, f in enumerate((flt_src, flt_dst)):
                for k in range(8):
                    i = t_.transpose(ps[0:T, 2 * s_ + k // 4, (k % 4) * 100:(k % 4) * 100 + 100], f[:, k, :], I[0:100, 0:100])
            i.then_inc(ids_ps, 1)
            pe.wait_ge(lim_ready, 1)
            for m in range(2):
                for k in range(8):
                    i = mm(ps[0:NT, 4 + 2 * m + k // 4, (k % 4) * 100:(k % 4) * 100 + 100],
                           chunk_lim[:, m, k:k + 1].to_broadcast([100, NT]), I[0:100, 0:100])
            i.then_inc(lims_ps, 1)
            pe.wait_ge(range_cols, 1)
            pe.wait_ge(ids_ready, 1)
            mm(ps[0:NT, 0, 0:1], lower, wcol[:, 5:6]).then_inc(base_ps, 1)
            pe.wait_ge(tabc_ready, 1)
            for m in range(3):
                i = mm(ps[0:1, 1, m * NT:m * NT + NT], wcol[:, 6 + m:7 + m] if m == 0 else wcol[:, 6 + m:7 + m], I[0:NT, 0:NT])
            i.then_inc(tab_ps, 1)
            pe.wait_ge(tab_ready, 1)
            pe.wait_ge(iotas, 2)

            def zero_banks(start):
                for b in range(BANKS):
                    n_ = 500 if b < 6 else T
                    i_ = mm(ps[0:T, b, 0:n_], zeros[:, 0:T], zeros[:, 0:n_], start, not start, True)
                return i_

            with pe.Fori(0, NT) as w:
                k0, k1 = (tab_load(pe, i, w) for i in range(2))
                pe.wait_ge(adj_by_act, w)
                pe.wait_ge(adj_by_dve, w)
                zero_banks(True)
                with pe.Fori(k0, k1) as k:
                    for c in range(PAIR):
                        pe.wait_ge(oh_ready, k * PAIR + c + 1)
                        for j in range(NT):
                            b, c0 = bank_cols(j)
                            i = mm(ps[0:T, b, c0:c0 + T], onehot_src[:, c, j * T:j * T + T], onehot_dst[:, c, :], False, False, True)
                        i.then_inc(oh_used, 1)
                zero_banks(False).then_inc(adj_summed, 1)
                pe.wait_ge(last_chain, w + k1 * PAIR + 1)
                pe.wait_ge(last_col, w)
                t_.transpose(ps[0:T, 7, 0:T], lastmax, I[0:T, 0:T]).then_inc(last_turned, 1)

            def transpose_nodes(s, feat, fin):
                for j in range(NT):
                    b, c0 = bank_cols(j)
                    i_ = t_.transpose(ps[0:fin, b, c0:c0 + T], feat[:, j, 0:fin], I[0:T, 0:T])
                i_.then_inc(s["ft_ps"], 1)

            def sage_layer(k):
                s, c = sage, sage_before(k)
                transpose_nodes(s, X, D)
                pe.wait_ge(s["ft_ready"], c["ft_ready"] + 1)
                if k == 0:
                    pe.wait_ge(eaug_ready, 1)
                    pe.wait_ge(ld_w0, 16 * 5)
                else:
                    pe.wait_ge(s["ld"], c["ld"] + 16 * 3)
                for b in range(NB):
                    pe.wait_ge(s["root_added"], c["root_added"] + b)
                    if k == 0:
                        for i in range(BT):
                            bank, c0 = block_cols(i)
                            last = t_.transpose(ps[0:17, bank, c0:c0 + T], eaug[:, b * BT + i, :], I[0:T, 0:T])
                        last.then_inc(s["et_ps"], 1)
                        pe.wait_ge(s["et_ready"], c["et_ready"] + b + 1)
                    for i in range(BT):
                        j = b * BT + i
                        o_ = ps[0:T, 2, i * D:i * D + D]
                        mm(o_, ft[0:D, j * T:j * T + T], wbuf[0:D, 64:128], True, False)
                        if k == 0:
                            mm(o_, aggT[0:17, i * T:i * T + T], wbuf[0:17, 128:192], False, False)
                        last = mm(o_, ones[0:1, 0:T], wbuf[0:1, 192:256], False, True)
                    last.then_inc(s["root_ps"], 1)
                pe.sem_inc(s["tile_used"], SLOTS)
                with pe.Fori(0, NB) as b:
                    pe.wait_ge(s["agg_out"], c["agg_out"] + b)
                    for j in range(NT):
                        pe.wait_ge(s["tile_ready"], c["tile_ready"] + b * NT + j + 1)
                        for bank, c0, n_ in PIECES:
                            last = mm(ps[0:D + 1, bank, 0:n_], X[:, j, :], slots[:, j % SLOTS, c0:c0 + n_], j == 0, j == NT - 1)
                        last.then_inc(s["tile_used"], 1)
                    pe.wait_ge(s["agg_out"], c["agg_out"] + b + 1)
                    for i in range(BT):
                        pe.wait_ge(s["proj_used"], c["proj_used"] + 3 * (b * BT) + max(3 * (i - 1), 0) + 2)
                        mm(ps[0:T, 6 + i % 2, 0:D], aggT[0:D, i * T:i * T + T], wbuf[0:D, 0:64])
                        mm(ps[0:T, 6 + i % 2, 128:129], aggT[0:D + 1, i * T:i * T + T], I[0:D + 1, D:D + 1]).then_inc(s["proj_ps"], 1)

            pe.wait_ge(ld_x, 16)
            pe.wait_ge(adj_by_act, NT)
            pe.wait_ge(adj_by_dve, NT)
            pe.wait_ge(last_col, NT)
            sage_layer(0)
            for li, (n, fin, heads, fo) in enumerate(GAT):
                s, c = gat, gat_before(li)
                H2 = 2 * heads
                if li == 0:
                    pe.wait_ge(x_ready, 1)
                else:
                    pe.wait_ge(bn["hid_ready"], li)
                transpose_nodes(s, X if n == "a" else hid, fin)
                pe.wait_ge(s["v_ready"], c["v_ready"] + 1)
                pe.wait_ge(s["ft_ready"], c["ft_ready"] + 1)
                for j in range(NT):
                    l = ft[0:fin, j * T:j * T + T]
                    if n == "c":
                        mm(ps[0:T, j // 8, (j % 8) * D:(j % 8) * D + D], l, wbuf[0:fin, 0:D])
                    last = mm(ps[0:T, 7, j * H2:j * H2 + H2], l, small[0:fin, 0:H2])
                last.then_inc(s["att_ps"], 1)
                pe.wait_ge(s["lim_cols"], c["lim_cols"] + 1)
                t_.transpose(ps[0:H2, 6, 0:T], small[0:T, 8:8 + H2], I[0:T, 0:T]).then_inc(s["lim_ps"], 1)
                pe.wait_ge(s["lim_rows"], c["lim_rows"] + 1)
                mm(ps[0:T, 5, 0:H2], small[0:H2, 16:17].to_broadcast([H2, T]), I[0:H2, 0:H2]).then_inc(s["lim_all"], 1)
                if n == "c":
                    pe.wait_ge(s["att_ready"], c["att_ready"] + 2)
                with pe.Fori(0, heads) as h:
                    pe.wait_ge(s["seen_step"], c["seen_step"] + h * NT + NT)
                    pe.wait_ge(s["seen_max"], c["seen_max"] + h)
                    for j in range(NT):
                        b, c0 = bank_cols(j)
                        last = t_.transpose(ps[0:T, b, c0:c0 + T], seen[:, j * T:j * T + T], I[0:T, 0:T])
                    last.then_inc(s["seen_turned"], 1)
                pe.wait_ge(s["cols_ready"], c["cols_ready"] + 1)
                pe.wait_ge(s["w_zero"], 1)
                with pe.Fori(0, NB) as b:
                    with pe.Fori(0, heads) as h:
                        q = b * heads + h
                        for r in range(2):
                            pe.wait_ge(s["diag_ready"], c["diag_ready"] + 2 * q + r + 1)
                            pe.wait_ge(s["row_ready"], c["row_ready"] + 2 * q + r)
                            for i in range(BT):
                                bank, c0 = block_cols(i)
                                last = mm(ps[0:T, 4 + bank, c0:c0 + T], ones[0:T, 0:T], diag[:, i, :])
                            last.then_inc(s["row_ps"], 1)
                        pe.wait_ge(s["agg_out"], c["agg_out"] + q)
                        for j in range(NT):
                            pe.wait_ge(s["tile_ready"], c["tile_ready"] + q * NT + j + 1)
                            for bank, c0, n_ in PIECES:
                                w_ = slots[:, j % SLOTS, c0:c0 + n_]
                                if n == "b":
                                    mm(ps[0:128, bank, 0:n_], hid[:, j, :], w_, j == 0, j == NT - 1)
                                    last = mm(ps[0:1, 2 + bank, 0:n_], ones[0:T, 0:1], w_, j == 0, j == NT - 1)
                                else:
                                    last = mm(ps[0:D + 1, bank, 0:n_], (X if n == "a" else h3)[:, j, :], w_, j == 0, j == NT - 1)
                            last.then_inc(s["tile_used"], 1)
                        pe.wait_ge(s["agg_out"], c["agg_out"] + q + 1)
                        for i in range(BT):
                            pe.wait_ge(s["proj_used"], c["proj_used"] + 2 * q * BT + max(2 * (i - 1), 0) + 2)
                            o_ = ps[0:T, 6 + i % 2, :]
                            tile = slice(i * T, i * T + T)
                            if n == "c":
                                mm(o_[:, 0:D], aggT[0:D, tile], I[0:D, 0:D])
                            else:
                                k_ = 128 if n == "b" else D + 1
                                mm(o_[:, 0:128], aggT[0:k_, tile], wbuf[0:k_, ds(h * 128, 128)])
                            if n == "b":
                                last = mm(o_[:, 128:129], dent[0:1, tile], ones[0:1, 0:1])
                            else:
                                last = mm(o_[:, 128:129], aggT[0:D + 1, tile], I[0:D + 1, D:D + 1])
                            last.then_inc(s["proj_ps"], 1)
                if n != "c":
                    t, tc = bn, bn_before(li)
                    pe.wait_ge(s["proj_used"], c["proj_used"] + 2 * NB * heads * BT + 2)
                    pe.wait_ge(s["back"], c["back"] + 16)
                    for j in range(NT):
                        last = mm(ps[0:T, 0, 0:128], ones[0:T, 0:T], hid[:, j, :], j == 0, j == NT - 1)
                    last.then_inc(t["sum_ps"], 1)
                    pe.wait_ge(t["sq_ready"], tc["sq_ready"] + 1)
                    for j in range(NT):
                        last = mm(ps[0:T, 1, 0:128], ones[0:T, 0:T], scratch[0:T, j * 128:j * 128 + 128], j == 0, j == NT - 1)
                    last.then_inc(t["var_ps"], 1)
            pe.wait_ge(x_ready, 2)
            sage_layer(1)
            s = m3
            pe.wait_ge(x_ready, 3)
            transpose_nodes(s, X, D)
            pe.wait_ge(s["ld"], 16 * 12)
            w2 = w3l[0:D, 256:768].rearrange("p (m b) -> p b m", b=8)
            for b in range(8):
                last = t_.transpose(ps[0:D, 7, b * D:b * D + D], w2[:, b, :], I[0:D, 0:D])
            last.then_inc(s["w2T_ps"], 1)
            pe.wait_ge(s["w2T_ready"], 1)
            for b in range(8):
                last = mm(ps[0:D, 7, b * D:b * D + D], w2T[:, b, :], w3l[0:D, 192:256])
            last.then_inc(s["wc_ps"], 1)
            pe.wait_ge(s["ft_ready"], 1)
            for b in range(BANKS):
                n_ = 500 if b < 6 else T
                last = mm(ps[0:D, b, 0:n_], w3l[0:D, 0:64], ft[0:D, b * 500:b * 500 + n_])
            last.then_inc(s["p1_ps"], 1)
            pe.wait_ge(s["p1_ready"], 1)
            for j in range(NT):
                o_ = ps[0:T, j // 4, (j % 4) * 128:(j % 4) * 128 + 128]
                mm(o_, p1T[:, j * T:j * T + T], w3l[0:D, 64:192], True, False, True)
                last = mm(o_[:, D:2 * D], ones[0:1, 0:T], w3l[0:1, 896:960], False, True, True)
            last.then_inc(s["qr_ps"], 1)
            pe.wait_ge(s["qr_ready"], 1)
            pe.wait_ge(s["wc_ready"], 1)

            pe.sem_inc(s["hT_ps"], GS)
            with pe.Fori(0, NCH // 8) as i8:

                def make_hT(k):
                    pe.wait_ge(gathered[k], 32 * i8 + 32)
                    if k >= 2:
                        pe.wait_ge(s["hT_ready"], 8 * i8 + k - 1)
                    else:
                        pe.wait_ge(s["hT_ready"], 8 * i8)
                    mm(ps[0:D, k % 2, 0:T], gath[:, k, 0, :], I[0:T, 0:T], True, False)
                    mm(ps[0:D, k % 2, 0:T], gath[:, k, 1, :], I[0:T, 0:T], False, True).then_inc(s["hT_ps"], 1)

                make_hT(0)
                for k in range(8):
                    t = 8 * i8 + k
                    if k < 7:
                        make_hT(k + 1)
                    pe.wait_ge(s["hT_ready"], t + 1)
                    pe.wait_ge(s["prod_ready"], t)
                    mm(ps[0:T, 2 + k % 2, :], hT[:, k % 4, :], wc.rearrange("p b c -> p (b c)")).then_inc(s["g_ps"], 1)
            pe.wait_ge(s["prod_ready"], NCH + 1)
            pe.wait_ge(s["iota"], 2)
            pe.sem_inc(s["oh_used"], 16)

            def zero_sum(start):
                for b in range(BANKS):
                    n_ = 500 if b < 6 else T
                    i_ = mm(ps[:, b, 0:n_], zero16[:, 0:128], zero16[:, 0:n_], start, not start, True)
                return i_

            zero_sum(True)
            with pe.Fori(0, NCH // 16) as i16:
                for k in range(16):
                    if k % 4 == 0:
                        pe.wait_ge(v_loaded[k // 4], 16 * i16 + 16)
                    pe.wait_ge(s["oh_ready"], 16 * i16 + k + 1)
                    for b in range(BANKS):
                        n_ = 500 if b < 6 else T
                        last = mm(ps[:, b, 0:n_], vin[:, k // 4, k % 4, :], oh3[:, k % 4, b * 500:b * 500 + n_], False, False, True)
                    last.then_inc(s["oh_used"], 1)
            zero_sum(False).then_inc(s["sum_done"], 1)
            pe.wait_ge(s["sum_copied"], 1)
            pe.wait_ge(s["sel_ready"], 1)
            for j in range(NT):
                last = mm(ps[0:T, j // 8, (j % 8) * D:(j % 8) * D + D], msum[:, j * T:j * T + T], small[:, 0:D])
            last.then_inc(s["turned"], 1)


def kernel(**inputs):
    import numpy as np
    import concourse.bacc as bacc
    from concourse.bass_utils import run_bass_kernel_spmd

    nc = bacc.Bacc("TRN2", target_bir_lowering=False, num_devices=1)
    arrays, params = {}, {}
    for name, value in inputs.items():
        a = np.ascontiguousarray(value)
        arrays[f"in_{name}"] = a
        params[name] = nc.dram_tensor(f"in_{name}", a.shape, mybir.dt.from_np(a.dtype), kind="ExternalInput").ap()
    out = nc.dram_tensor("out", (N, D), F32, kind="ExternalOutput").ap()
    build_gnn(nc, params, out)
    got = run_bass_kernel_spmd(nc, [arrays], core_ids=[0])
    return got.results[0]["out"]
```

```python
from contextlib import ExitStack

import concourse.bass as bass
from concourse import mybir

F32 = mybir.dt.float32
F16 = mybir.dt.float16
BF16 = mybir.dt.bfloat16
U16 = mybir.dt.uint16
I32 = mybir.dt.int32
ALU = mybir.AluOpType
ACT = mybir.ActivationFunctionType
X_AXIS = mybir.AxisListType.X
ds = bass.ds

N = 3125
T = 125
NT = N // T
D = 64
E = 100000
NCH = E // T
PAIR = 2
NG = NCH // PAIR
BT = 5
NB = NT // BT
BW = BT * T
SLOTS = 5
HEADS = 4
NEG = 0.2
EPS = 1e-5
POOL_SLOTS = {"a": (0, 2, 3), "b": (0, 2), "c": (0, 2, 3)}
POOL_TILES = {n: NT // SLOTS * len(slots) for n, slots in POOL_SLOTS.items()}
DVE_TILES = {n: NT - tiles for n, tiles in POOL_TILES.items()}
LAG = 8
NEAR = 2500
BANKS = 7

GAT = (("a", D, HEADS, 128), ("b", 128, HEADS, 128), ("c", 128, 1, D))


def build_gnn(nc, p, out):
    with ExitStack() as ctx:
        def sb(name, shape, dt=F32):
            return ctx.enter_context(nc.sbuf_tensor(name, shape, dt))

        def sem(name):
            return ctx.enter_context(nc.semaphore(name))

        adj = sb("adj", [T, NT * N + 3], U16)
        adj3 = adj[:, 0:NT * N].rearrange("p (j d) -> p j d", j=NT)
        scratch = sb("scratch", [128, 3200])
        hwork = sb("hwork", [128, 3225])
        work = sb("work", [128, 2 * BW + BW + BT * 128 + BT * 129])
        rows = work[:, 0:2 * BW].rearrange("p (r d) -> p r d", r=2)
        aggT = work[:, 2 * BW:3 * BW]
        acc = work[0:T, 3 * BW:3 * BW + BT * 128].rearrange("p (i c) -> p i c", i=BT)
        agg_sums = work[0:T, 3 * BW + BT * 128:]
        X = sb("X", [T, NT, D + 1])
        edge_ids = sb("edge_ids", [T, 2, NCH], U16)
        wbuf = sb("wbuf", [128, 640])
        att = sb("att", [T, NT, 8])
        cols = sb("cols", [T, 4, NT, HEADS])
        dst_cols = sb("dst_cols", [T, 2, NT * HEADS + BT])
        ident = sb("ident", [128, 128])
        ones = sb("ones", [128, 128])
        small = sb("small", [128, 64])
        table = sb("table", [1, 3 * NT], I32)
        last_edge = sb("last_edge", [T, NT])
        ps = ctx.enter_context(nc.psum_tensor("ps", [128, 8, 512], F32))

        rflat = work[:, 0:2 * BW]
        hflat = hwork[:, :]
        raw_src = rflat[0:100, 0:1000].bitcast(I32).rearrange("q (k e) -> q k e", k=8)
        raw_dst = scratch[0:100, 0:1000].bitcast(I32).rearrange("q (k e) -> q k e", k=8)
        flt_src = scratch[0:100, 1000:2000].rearrange("q (k e) -> q k e", k=8)
        flt_dst = scratch[0:100, 2000:3000].rearrange("q (k e) -> q k e", k=8)
        chunk_lim = hflat[0:100, 0:16].rearrange("q (m k) -> q m k", m=2)
        gmax = hflat[0:NT, 16:416]
        gmin = hflat[0:NT, 416:816]
        rev = hflat[0:NT, 816:1216]
        fwd = hflat[0:NT, 1216:1616]
        tmpg = hflat[0:NT, 1616:2016]
        lower = hflat[0:NT, 2016:2041]
        wcol = hflat[0:NT, 2041:2051]
        eid = rflat[0:T, 0:NCH]
        onehot_src = scratch[0:T, 0:3126].bitcast(BF16).rearrange("p (c n) -> p c n", c=2)[:, :, 0:N]
        iota = hflat[0:T, 0:1563].bitcast(U16)[:, 0:N]
        zeros = hflat[0:T, 1563:1819].bitcast(BF16)
        onehot_dst = hflat[0:T, 1819:1945].bitcast(BF16).rearrange("p (c n) -> p c n", c=2)[:, :, 0:T]
        lastmax = work[0:T, 3 * BW:3 * BW + T]
        ft = scratch[:, 0:N]
        slots = scratch[0:T, 0:SLOTS * BW].rearrange("p (s d) -> p s d", s=SLOTS)
        res = hflat[0:T, 1625:3225].rearrange("p (j c) -> p j c", j=NT)
        h3 = hflat[0:T, 0:1625].rearrange("p (j c) -> p j c", j=NT)
        hid = hflat[0:T, 0:3225].rearrange("p (j c) -> p j c", j=NT)
        seen = scratch[0:T, 0:N]
        ea = hflat[0:T, 0:400].rearrange("p (j c) -> p j c", j=NT)
        eaug = hflat[0:T, 400:825].rearrange("p (j c) -> p j c", j=NT)
        eidx = hflat[0:T, 825:850].bitcast(I32)
        pool_counts = {"b": [work[0:T, 3 * BW:4 * BW]], "c": [hflat[0:T, 1640 + i * BW:1640 + i * BW + BW] for i in range(2)]}
        pool_counts["a"] = pool_counts["c"]
        diag = edge_ids[:].rearrange("p a b -> p (a b)")[:, 0:2 * BW].bitcast(F32).rearrange("p (i d) -> p i d", i=BT)
        gat_out = {n: nc.dram_tensor(f"gat_out_{n}", (N, fo), F32, kind="Internal").ap() for n, _, _, fo in GAT}
        q_dram = nc.dram_tensor("q_dram", (N, D), F32, kind="Internal").ap()
        r_dram = nc.dram_tensor("r_dram", (N, D), F32, kind="Internal").ap()
        v_dram = nc.dram_tensor("v_dram", (NCH // 4, T, 4 * 128), F16, kind="Internal").ap()

        big = adj[:].bitcast(F32)

        def at(off, parts, words):
            return big[0:parts, off:off + words]

        o = 0
        basis = at(o, T, 6400).rearrange("p (t b) -> p t b", b=8); o += 6400
        idx3 = at(o, T, 1600).bitcast(I32).rearrange("p (s t) -> p s t", s=2); o += 1600
        src3 = at(o, T, (NCH + LAG) // 2).bitcast(U16); o += (NCH + LAG) // 2
        p1T = at(o, D, N); o += N
        qr = at(o, T, 3200).rearrange("p (j c) -> p j c", j=NT); o += 3200
        GS = 8
        gath = at(o, T, GS * 128).rearrange("p (s c) -> p s c", s=GS); o += GS * 128
        pairT = work[:, 512:512 + 4 * T].rearrange("p (s e) -> p s e", s=4)
        prod = at(o, T, 2 * 9 * D).rearrange("p (s b c) -> p s b c", s=2, b=9); o += 2 * 9 * D
        uval = at(o, T, 2 * 4 * D).rearrange("p (s q c) -> p s q c", s=2, q=4); o += 2 * 4 * D
        vval = at(o, T, 2 * 4 * D).rearrange("p (s q c) -> p s q c", s=2, q=4); o += 2 * 4 * D
        vsplit = at(o, T, 2 * 256).bitcast(F16).rearrange("p (s q h c) -> p s q h c", s=2, q=4, h=2); o += 512
        w2T = at(o, D, 8 * 128).rearrange("p (b k) -> p b k", b=8); o += 8 * 128
        wc = work[:, 0:512]
        w3l = hflat[:, 0:1024]
        idx_now = at(o, T, 4 * GS).bitcast(I32).rearrange("p (h s t) -> p h s t", h=2, s=2); o += 4 * GS
        zero16 = at(o, T, 256).bitcast(F16); o += 256
        iota3 = at(o, T, 1563).bitcast(U16)[:, 0:N]; o += 1563
        oh3 = at(o, T, 4 * 1563).bitcast(F16).rearrange("p (s n) -> p s n", s=4)[:, :, 0:N]; o += 4 * 1563
        vin = at(o, T, 4 * 256).bitcast(F16).rearrange("p (s q c) -> p s q c", s=4, q=4); o += 4 * 256
        msum = scratch[:, 0:N]
        assert o <= (NT * N + 3) // 2, o

        ld_edges, ld_x, ld_w0 = sem("ld_edges"), sem("ld_x"), sem("ld_w0")
        consts, iotas, eids, idx_float, lim_ready = sem("consts"), sem("iotas"), sem("eids"), sem("idx_float"), sem("lim_ready")
        ids_ps, lims_ps, ids_ready, range_cols, base_ps, tabc_ready, tab_ps, tab_ready = (
            sem("ids_ps"), sem("lims_ps"), sem("ids_ready"), sem("range_cols"), sem("base_ps"),
            sem("tabc_ready"), sem("tab_ps"), sem("tab_ready"))
        oh_ready, oh_used, ohd_built, last_chain = sem("oh_ready"), sem("oh_used"), sem("ohd_built"), sem("last_chain")
        adj_summed, last_turned, last_col = sem("adj_summed"), sem("last_turned"), sem("last_col")
        adj_by_act, adj_by_dve = sem("adj_by_act"), sem("adj_by_dve")
        chain, table_loaded = sem("dve_chain"), sem("act_table_loaded")
        x_ready, x_var, x_std = sem("x_ready"), sem("x_var"), sem("x_std")
        eidx_ready, ea_ready, eaug_ready = sem("eidx_ready"), sem("ea_ready"), sem("eaug_ready")
        sage = {k: sem(f"sage_{k}") for k in (
            "ft_ps", "ft_ready", "et_ps", "et_ready", "root_ps", "root_added", "tile_ready", "tile_used",
            "agg_out", "proj_ps", "proj_used", "ld")}
        gat = {k: sem(f"gat_{k}") for k in (
            "ld", "v_ready", "ft_ps", "ft_ready", "att_ps", "att_ready", "lim_cols", "lim_ps", "lim_rows", "lim_all",
            "counts_ready", "pool_turn", "act_turn", "seen_step", "seen_turned", "seen_max", "cols_ready",
            "diag_ready", "row_ps", "row1_ready", "row2_ready", "acc_zero",
            "shifted", "exped", "tile_by_dve", "tile_by_pool", "tile_used", "agg_copied", "den_ready", "scaled",
            "aggT_ps", "aggT_ready", "proj_ps", "block_ready", "stored", "block_stored", "back")}
        bn = {k: sem(f"bn_{k}") for k in (
            "ld", "sum_ps", "sq_ready", "var_ps", "var_ready", "std_ready", "min_ready", "exp_ready", "hid_ready")}

        def sage_before(k):
            per = dict.fromkeys(sage, 1) | {
                "et_ps": NB, "et_ready": NB, "root_ps": NB, "root_added": NB, "tile_ready": NT * NB,
                "tile_used": NT * NB + SLOTS, "agg_out": NB, "proj_ps": NB, "proj_used": 3 * NB, "ld": 0}
            return {name: k * count + (name != "ld") for name, count in per.items()}

        def gat_before(li):
            total = {name: int(name not in ("ld", "stored", "back")) for name in gat}
            for n, _, heads, _ in GAT[:li]:
                q = NB * heads
                per = dict.fromkeys(gat, q) | dict.fromkeys(
                    ("v_ready", "ft_ps", "ft_ready", "att_ps", "lim_cols", "lim_ps", "lim_rows", "lim_all",
                     "cols_ready"), 1) | {
                    "ld": 16 * 4, "att_ready": 0, "seen_step": heads * NT, "seen_turned": heads, "seen_max": heads,
                    "diag_ready": 2 * (q + 1), "row_ps": 2 * (q + 1), "row1_ready": q + 1, "row2_ready": q + 1,
                    "shifted": q * NT, "exped": q * NT, "tile_by_dve": q * DVE_TILES[n], "tile_by_pool": q * POOL_TILES[n],
                    "counts_ready": q * POOL_TILES[n],
                    "tile_used": q * NT + SLOTS, "block_ready": NB, "block_stored": NB, "stored": 16 * NB, "back": 16} | (
                    {"acc_zero": 0} if n == "b" else {"acc_zero": NB, "aggT_ps": 0, "aggT_ready": 0})
                total = {name: total[name] + per[name] for name in total}
            return total

        def bn_before(li):
            return {name: li * (32 if name == "ld" else 1) for name in bn}

        m3 = {k: sem(f"m3_{k}") for k in (
            "ld", "src_ready", "w2T_ps", "w2T_ready", "wc_ps", "wc_ready", "ft_ps", "ft_ready", "p1_ps", "p1_ready", "qr_ps", "qr_ready",
            "stored", "pairT_ps", "pairT_ready", "g_ps", "prod_ready", "u_ready", "v_ready", "hi_ready",
            "lo_ready", "v_stored", "oh_ready", "oh_used", "far_oh_ready", "far_oh_used", "near_done", "near_copied",
            "sum_done", "sum_copied", "turned", "out_stored", "iota", "v_free", "sel_ready", "idx_now", "pool_turn")}
        gathered = [sem(f"gathered_{k}") for k in range(GS)]
        v_loaded = [sem(f"v_loaded_{k}") for k in range(4)]

        def bank_cols(j):
            return j // 4, (j % 4) * T

        def block_cols(i):
            return (0, i * T) if i < 3 else (1, (i - 3) * T)

        def tile_rank(n, j):
            mine = [k for k in range(j + 1) if (k % SLOTS in POOL_SLOTS[n]) == (j % SLOTS in POOL_SLOTS[n])]
            return len(mine)

        def counts_of(n, j):
            return pool_counts[n][tile_rank(n, j) % len(pool_counts[n])]

        COPY_AT, DEN_AT, SCALE_AT, TURN_AT, AGGT_AT, PROJ_AT = 1, 5, 7, 8, 10, 12
        NARROW_PROJ_AT, NARROW_ADD_AT, ZERO_AT = 3, 10, 16
        DIAG_AT, ROW_AT = (8, 14), (10, 16)
        PIECES = ((0, 0, 3 * T), (1, 3 * T, 2 * T))

        block = ctx.enter_context(nc.Block())

        def tab_load(eng, which, w):
            return eng.value_load(table[0:1, ds(w + which * NT, 1)], min_val=0, max_val=NT * NG)

        @block.sync
        def _(sp):
            sp.dma_start(raw_src, p["src"].rearrange("(k q e) -> q k e", k=8, q=100)).then_inc(ld_edges, 16)
            sp.dma_start(raw_dst, p["dst"].rearrange("(k q e) -> q k e", k=8, q=100)).then_inc(ld_edges, 16)
            for counts, others in ((sage, ("ld",)), (gat, ("ld", "stored", "back"))):
                for name, count in counts.items():
                    if name not in others:
                        sp.sem_inc(count, 1)
            for count in (adj_by_act, adj_by_dve, last_turned, last_col, m3["pairT_ready"], m3["u_ready"]):
                sp.sem_inc(count, 1)
            sp.dma_start(X[:, :, 0:D], p["x"].rearrange("(j q) c -> q j c", q=T)).then_inc(ld_x, 16)
            sp.dma_start(wbuf[0:D, 0:64], p["L0_gnn_W_l"]).then_inc(ld_w0, 16)
            sp.dma_start(wbuf[0:D, 64:128], p["L0_gnn_W_r"]).then_inc(ld_w0, 16)
            sp.dma_start(wbuf[0:16, 128:192], p["L0_gnn_W_e"]).then_inc(ld_w0, 16)
            sp.dma_start(wbuf[16:17, 128:192], p["L0_gnn_b_e"].rearrange("(a c) -> a c", a=1)).then_inc(ld_w0, 16)
            sp.dma_start(wbuf[0:1, 192:256], p["L0_gnn_b_l"].rearrange("(a c) -> a c", a=1)).then_inc(ld_w0, 16)
            for li, (n, fin, heads, fo) in enumerate(GAT):
                s, c = gat, gat_before(li)
                W, a_s, a_d, bias = (p[f"L1_gnn_{k}{li + 1}"] for k in ("W", "as", "ad", "b"))
                if li == 0:
                    sp.wait_ge(x_ready, 1)
                else:
                    sp.wait_ge(bn["hid_ready"], li)
                wn = heads * fo
                sp.dma_start(wbuf[0:fin, 0:wn], W).then_inc(s["ld"], 16)
                sp.dma_start(scratch[0:fin, 0:wn], a_s.rearrange("h c -> (h c)").partition_broadcast(fin)).then_inc(s["ld"], 16)
                sp.dma_start(scratch[0:fin, 512:512 + wn], a_d.rearrange("h c -> (h c)").partition_broadcast(fin)).then_inc(s["ld"], 16)
                sp.dma_start(wbuf[0:T, 512:512 + fo], bias.partition_broadcast(T)).then_inc(s["ld"], 16)
                gout = gat_out[n].rearrange("(j q) c -> q j c", q=T)
                with sp.Fori(0, NB) as b:
                    sp.wait_ge(s["block_ready"], c["block_ready"] + b + 1)
                    sp.dma_start(gout[:, ds(b * BT, BT), :], acc[:, :, 0:fo]).then_inc(s["stored"], 16)
                    sp.wait_ge(s["stored"], c["stored"] + 16 * (b + 1))
                    sp.sem_inc(s["block_stored"], 1)
                sp.wait_ge(s["stored"], c["stored"] + 16 * NB)
                if n == "c":
                    sp.dma_start(scratch[0:T, 0:NT * fo].rearrange("p (j c) -> p j c", j=NT), gout).then_inc(s["back"], 16)
                else:
                    sp.dma_start(hid[:, :, 0:128], gout).then_inc(s["back"], 16)
                    for i, k in enumerate(("g", "be")):
                        sp.dma_start(rflat[0:T, i * 128:i * 128 + 128],
                                     p[f"L1_gnn_{k}{li + 1}"].partition_broadcast(T)).then_inc(bn["ld"], 16)
            sp.wait_ge(x_ready, 2)
            s, c = sage, sage_before(1)
            sp.dma_start(wbuf[0:D, 0:64], p["L2_gnn_W"][D:2 * D, :]).then_inc(s["ld"], 16)
            sp.dma_start(wbuf[0:D, 64:128], p["L2_gnn_W"][0:D, :]).then_inc(s["ld"], 16)
            sp.dma_start(wbuf[0:1, 192:256], p["L2_gnn_b"].rearrange("(a c) -> a c", a=1)).then_inc(s["ld"], 16)
            s = m3
            sp.wait_ge(x_ready, 3)
            sp.dma_start(idx3[:, 0, :], p["src"].rearrange("(q t) -> q t", q=T)).then_inc(s["ld"], 16)
            sp.dma_start(idx3[:, 1, :], p["dst"].rearrange("(q t) -> q t", q=T)).then_inc(s["ld"], 16)
            sp.dma_start(basis, p["edge_attr_8"].rearrange("(q t) b -> q t b", q=T)).then_inc(s["ld"], 16)
            sp.dma_start(w3l[0:D, 0:64], p["L3_gnn_pp_W"]).then_inc(s["ld"], 16)
            sp.dma_start(w3l[0:D, 64:128], p["L3_gnn_pi_W1"][0:D, :]).then_inc(s["ld"], 16)
            sp.dma_start(w3l[0:D, 128:192], p["L3_gnn_pi_W1"][D:2 * D, :]).then_inc(s["ld"], 16)
            sp.dma_start(w3l[0:D, 192:256], p["L3_gnn_ii_W"]).then_inc(s["ld"], 16)
            sp.dma_start(w3l[0:D, 256:768], p["L3_gnn_pi_W2"]).then_inc(s["ld"], 16)
            sp.dma_start(w3l[0:D, 768:769], p["L3_gnn_pp_b"].rearrange("(c a) -> c a", a=1)).then_inc(s["ld"], 16)
            sp.dma_start(w3l[0:1, 896:960], p["L3_gnn_pi_b1"].rearrange("(a c) -> a c", a=1)).then_inc(s["ld"], 16)
            for k in range(2):
                sp.dma_start(prod[:, k, 8, :], p["L3_gnn_ii_b"].partition_broadcast(T)).then_inc(s["ld"], 16)
            sp.sem_inc(s["v_free"], 2)
            sp.wait_ge(s["qr_ready"], 1)
            sp.dma_start(q_dram.rearrange("(j q) c -> q j c", q=T), qr[:, :, 0:D]).then_inc(s["stored"], 16)
            sp.dma_start(r_dram.rearrange("(j q) c -> q j c", q=T), qr[:, :, D:2 * D]).then_inc(s["stored"], 16)
            with sp.Fori(0, NCH // 8) as i:
                for k in range(2):
                    sp.wait_ge(s["lo_ready"], 2 * i + k + 3)
                    sp.dma_start(v_dram[ds(2 * i + k, 1), :, :].rearrange("a q c -> q (a c)"),
                                 vsplit[:, k].rearrange("p q h c -> p (q h c)")).then_inc(s["v_stored"], 16)
                    sp.wait_ge(s["v_stored"], 16 * (2 * i + k) + 16)
                    sp.sem_inc(s["v_free"], 1)
            with sp.Fori(0, NCH // 16) as i:
                for k in range(4):
                    sp.wait_ge(s["far_oh_used"], 4 * (4 * i + k) + 4)
                    sp.dma_start(vin[:, k], v_dram[ds(4 * i + k, 1), :, :].rearrange("a q (g c) -> q (a g) c", g=4)).then_inc(v_loaded[k], 16)
            sp.wait_ge(x_ready, 4)
            sp.dma_start(out.rearrange("(j q) c -> q j c", q=T), X[:, :, 0:D]).then_inc(s["out_stored"], 16)
            sp.wait_ge(s["out_stored"], 16)

        @block.gpsimd
        def _(pool):
            g = nc.gpsimd
            g.memset(ident[:], 0.0).then_inc(consts, 1)
            g.memset(ones[:], 1.0).then_inc(consts, 1)
            g.memset(lower, 1.0).then_inc(consts, 1)
            g.memset(X[:, :, D:D + 1], 1.0).then_inc(consts, 1)
            pool.wait_ge(consts, 4)
            g.affine_select(out=ident[:], in_=ident[:], compare_op=ALU.not_equal, fill=1.0, base=0,
                            pattern=[[-1, 128]], channel_multiplier=1).then_inc(consts, 1)
            g.affine_select(out=lower, in_=lower, compare_op=ALU.is_gt, fill=0.0, base=0,
                            pattern=[[1, NT]], channel_multiplier=-1).then_inc(consts, 1)
            g.iota(fwd, [[1, NG]], base=1, channel_multiplier=0, allow_small_or_imprecise_dtypes=True).then_inc(consts, 1)
            g.iota(rev, [[-1, NG]], base=NG, channel_multiplier=0, allow_small_or_imprecise_dtypes=True).then_inc(consts, 1)
            g.iota(wcol[:, 0:1], [[0, 1]], base=0, channel_multiplier=T, allow_small_or_imprecise_dtypes=True).then_inc(consts, 1)
            pool.wait_ge(idx_float, 2)
            g.iota(eid, [[T, NCH]], base=1, channel_multiplier=1, allow_small_or_imprecise_dtypes=True).then_inc(eids, 1)
            pool.wait_ge(tab_ready, 1)
            g.iota(iota, [[1, N]], base=0, channel_multiplier=0).then_inc(iotas, 1)
            g.memset(zeros, 0.0).then_inc(iotas, 1)
            pool.wait_ge(eidx_ready, 1)
            for j in range(NT):
                g.indirect_dma_start(ea[:, j, :], None, p["edge_attr_16"],
                                     bass.IndirectOffsetOnAxis(ap=eidx[:, j:j + 1], axis=0)).then_inc(ea_ready, 16)
            for li, (n, fin, heads, fo) in enumerate(GAT):
                s, c = gat, gat_before(li)

                def make_diag(p, r):
                    pool.wait_ge(s["row_ps"], c["row_ps"] + 2 * p + r)
                    pool.sem_inc(s["pool_turn"], 1)
                    g.tensor_tensor(diag, ident[0:T, 0:T].unsqueeze(1).to_broadcast([T, BT, T]),
                                    dst_cols[:, r, ds(p * BT, BT)].unsqueeze(2).to_broadcast([T, BT, T]), ALU.mult).then_inc(s["diag_ready"], 1)

                pool.wait_ge(s["cols_ready"], c["cols_ready"] + 1)
                for r in range(2):
                    make_diag(0, r)
                with pool.Fori(0, NB) as b:
                    with pool.Fori(0, heads) as h:
                        q = b * heads + h
                        for j in range(NT):
                            if j in DIAG_AT:
                                make_diag(q + 1, DIAG_AT.index(j))
                            if j % SLOTS in POOL_SLOTS[n]:
                                done = q * POOL_TILES[n] + tile_rank(n, j)
                                pool.wait_ge(s["counts_ready"], c["counts_ready"] + done)
                                pool.wait_ge(s["exped"], c["exped"] + q * NT + j + 1)
                                pool.sem_inc(s["pool_turn"], 1)
                                g.tensor_tensor(slots[:, j % SLOTS, :], slots[:, j % SLOTS, :], counts_of(n, j),
                                                ALU.mult).then_inc(s["tile_by_pool"], 1)
            s = m3
            pool.wait_ge(x_ready, 3)
            g.iota(iota3, [[1, N]], base=0, channel_multiplier=0).then_inc(s["iota"], 1)
            g.memset(zero16, 0.0).then_inc(s["iota"], 1)
            g.memset(vsplit, 0.0).then_inc(s["iota"], 1)
            pool.wait_ge(s["stored"], 32)
            pool.wait_ge(s["ld"], 16 * 12)
            with pool.Fori(0, NCH // (2 * GS)) as i:
                for half in range(2):
                    t0 = (2 * i + half) * GS
                    pool.wait_ge(s["pairT_ps"], t0 + 1)
                    pool.sem_inc(s["pool_turn"], 1)
                    g.tensor_copy(idx_now[:, half], idx3[:, :, ds(t0, GS)]).then_inc(s["idx_now"], 1)
                    pool.wait_ge(s["idx_now"], 2 * i + half + 1)
                    pool.sem_inc(s["pool_turn"], 1)
                    for k in range(GS):
                        pool.wait_ge(s["pairT_ps"], t0 + k + 1)
                        pool.sem_inc(s["pool_turn"], 1)
                        for a, table_dram in enumerate((q_dram, r_dram)):
                            g.indirect_dma_start(gath[:, k, a * D:a * D + D], None, table_dram,
                                                 bass.IndirectOffsetOnAxis(ap=idx_now[:, half, a, k:k + 1], axis=0)).then_inc(gathered[k], 16)

        @block.scalar
        def _(act):
            a = nc.scalar
            act.wait_ge(consts, 4)
            with act.Fori(0, NT) as w:
                a.copy(small[0:1, 60:61], ones[0:1, 0:1]).then_inc(table_loaded, 1)
                act.wait_ge(table_loaded, w + 1)
                act.wait_ge(adj_summed, w + 1)
                a.copy(adj3[:, 0:16, ds(w * T, T)].rearrange("p (b j) d -> p b j d", b=4),
                       ps[0:T, 0:4, 0:500].rearrange("p b (j d) -> p b j d", j=4)).then_inc(adj_by_act, 1)

            def copy_ft(s, fin, before):
                act.wait_ge(s["ft_ps"], before + 1)
                a.copy(ft[0:fin, 0:3000].rearrange("p (b d) -> p b d", b=6), ps[0:fin, 0:6, 0:500])
                a.copy(ft[0:fin, 3000:N], ps[0:fin, 6, 0:T]).then_inc(s["ft_ready"], 1)

            def layernorm_std(k):
                act.wait_ge(x_var, k)
                a.activation(rflat[0:T, 50:75], rflat[0:T, 25:50], ACT.Sqrt).then_inc(x_std, 1)

            def sage_layer(k):
                s, c = sage, sage_before(k)
                copy_ft(s, D, c["ft_ps"])
                if k == 0:
                    for b in range(NB):
                        act.wait_ge(s["et_ps"], c["et_ps"] + b + 1)
                        for bank, c0, n in PIECES:
                            i = a.copy(aggT[0:17, c0:c0 + n], ps[0:17, bank, 0:n])
                        i.then_inc(s["et_ready"], 1)
                act.wait_ge(s["root_ps"], c["root_ps"] + NB)
                with act.Fori(0, NB) as b:
                    for j in range(NT):
                        act.wait_ge(s["tile_used"], c["tile_used"] + b * NT + j + 1)
                        a.copy(slots[:, j % SLOTS, :], adj3[:, j, ds(b * BW, BW)]).then_inc(s["tile_ready"], 1)
                    act.wait_ge(s["tile_used"], c["tile_used"] + b * NT + NT + SLOTS)
                    act.wait_ge(s["proj_ps"], c["proj_ps"] + b)
                    for bank, c0, n in PIECES:
                        i = a.copy(aggT[0:D + 1, c0:c0 + n], ps[0:D + 1, bank, 0:n])
                    i.then_inc(s["agg_out"], 1)

            sage_layer(0)
            layernorm_std(1)
            for li, (n, fin, heads, fo) in enumerate(GAT):
                s, c = gat, gat_before(li)
                fin_ = 128 if n == "b" else D
                act.wait_ge(s["v_ready"], c["v_ready"] + 1)
                copy_ft(s, fin, c["ft_ps"])
                if n == "c":
                    act.wait_ge(s["att_ps"], c["att_ps"] + 1)
                    a.copy(h3[:, 0:24, 0:D].rearrange("p (b j) c -> p b j c", b=3),
                           ps[0:T, 0:3, :].rearrange("p b (j c) -> p b j c", j=8))
                    a.copy(h3[:, 24, 0:D], ps[0:T, 3, 0:D]).then_inc(s["att_ready"], 1)

                def copy_row1(p):
                    act.wait_ge(s["row_ps"], c["row_ps"] + 2 * p + 1)
                    act.wait_ge(s["shifted"], c["shifted"] + p * NT)
                    a.copy(rows[0:T, 0, 0:3 * T], ps[0:T, 2, 0:3 * T])
                    a.copy(rows[0:T, 0, 3 * T:BW], ps[0:T, 3, 0:2 * T]).then_inc(s["row1_ready"], 1)

                sums = agg_sums[:, 0:BT * (fin_ + 1)].rearrange("p (i c) -> p i c", i=BT)

                def copy_sums(q):
                    act.wait_ge(s["tile_used"], c["tile_used"] + q * NT + NT + SLOTS)
                    if n != "b":
                        act.wait_ge(s["proj_ps"], c["proj_ps"] + q)
                        for bank, c0, nn in PIECES:
                            i = a.copy(aggT[0:D + 1, c0:c0 + nn], ps[0:D + 1, bank, 0:nn])
                        i.then_inc(s["agg_copied"], 1)
                        return
                    act.wait_ge(s["aggT_ps"], c["aggT_ps"] + q)
                    for bank, i0, i1 in ((0, 0, 3), (1, 3, BT)):
                        i = a.copy(sums[:, i0:i1, :], ps[0:T, bank, 0:(i1 - i0) * (fin_ + 1)].rearrange("p (i c) -> p i c", i=i1 - i0))
                    i.then_inc(s["agg_copied"], 1)

                def scale_sums(q):
                    act.wait_ge(s["den_ready"], c["den_ready"] + q + 1)
                    for i in range(BT):
                        last = a.activation(sums[:, i, 0:fin_], sums[:, i, 0:fin_], ACT.Copy, scale=small[0:T, 40 + i:41 + i])
                    last.then_inc(s["scaled"], 1)

                def copy_aggT(q):
                    act.wait_ge(s["aggT_ps"], c["aggT_ps"] + q + 1)
                    act.wait_ge(s["proj_ps"], c["proj_ps"] + q)
                    for bank, c0, nn in PIECES:
                        i = a.copy(aggT[0:fin_, c0:c0 + nn], ps[0:fin_, 4 + bank, 0:nn])
                    i.then_inc(s["aggT_ready"], 1)

                def exps(b, h, after_first):
                    q = b * heads + h
                    for j in range(NT):
                        if j % SLOTS in POOL_SLOTS[n]:
                            act.wait_ge(s["tile_by_pool"], c["tile_by_pool"] + q * POOL_TILES[n] + max(tile_rank(n, j) - len(pool_counts[n]), 0))
                            act.sem_inc(s["act_turn"], 1)
                            a.copy(counts_of(n, j), adj3[:, j, ds(b * BW, BW)]).then_inc(s["counts_ready"], 1)
                        act.wait_ge(s["shifted"], c["shifted"] + q * NT + j + 1)
                        a.activation(slots[:, j % SLOTS, :], slots[:, j % SLOTS, :], ACT.Exp,
                                     bias=cols[:, 2, j, ds(h, 1)]).then_inc(s["exped"], 1)
                        if after_first and j == COPY_AT:
                            copy_sums(q - 1)
                        if after_first and n == "b" and j == SCALE_AT:
                            scale_sums(q - 1)
                        if after_first and n == "b" and j == AGGT_AT:
                            copy_aggT(q - 1)
                    copy_row1(q + 1)

                act.wait_ge(s["cols_ready"], c["cols_ready"] + 1)
                copy_row1(0)
                with act.Fori(0, NB) as b:
                    if n == "b":
                        act.wait_ge(s["block_stored"], c["block_stored"] + b)
                    exps(b, 0, False)
                    if heads > 1:
                        with act.Fori(1, heads) as h:
                            exps(b, h, True)
                    q_last = b * heads + heads - 1
                    copy_sums(q_last)
                    if n == "b":
                        scale_sums(q_last)
                        copy_aggT(q_last)
                if n != "c":
                    t, tc = bn, bn_before(li)
                    act.wait_ge(t["var_ready"], tc["var_ready"] + 1)
                    a.activation(rflat[0:T, 512:640], rflat[0:T, 384:512], ACT.Sqrt).then_inc(t["std_ready"], 1)
                    act.wait_ge(t["min_ready"], tc["min_ready"] + 1)
                    a.activation(scratch[0:T, 0:3200], scratch[0:T, 0:3200], ACT.Exp).then_inc(t["exp_ready"], 1)
            layernorm_std(2)
            sage_layer(1)
            layernorm_std(3)
            s = m3
            copy_ft(s, D, 0)
            act.wait_ge(s["w2T_ps"], 1)
            a.copy(w2T[:, :, 0:D], ps[0:D, 7, :].rearrange("p (b k) -> p b k", b=8))
            a.copy(w2T[:, :, D:128], ps[0:D, 7, :].rearrange("p (b k) -> p b k", b=8)).then_inc(s["w2T_ready"], 1)
            act.wait_ge(s["wc_ps"], 1)
            a.copy(wc, ps[:, 7, :]).then_inc(s["wc_ready"], 1)
            act.wait_ge(s["p1_ps"], 1)
            for b in range(BANKS):
                nn = 500 if b < 6 else T
                i = a.activation(p1T[:, b * 500:b * 500 + nn], ps[0:D, b, 0:nn], ACT.Tanh, bias=w3l[0:D, 768:769])
            i.then_inc(s["p1_ready"], 1)
            act.wait_ge(s["qr_ps"], 1)
            a.copy(qr[:, 0:24, :].rearrange("p (b j) c -> p b j c", b=6), ps[0:T, 0:6, :].rearrange("p b (j c) -> p b j c", j=4))
            a.copy(qr[:, 24, :], ps[0:T, 6, 0:128]).then_inc(s["qr_ready"], 1)
            act.sem_inc(s["v_ready"], 2)

            def messages(z, slot):
                act.wait_ge(s["u_ready"], 2 * z + 3)
                act.wait_ge(s["lo_ready"], z + 1)
                a.activation(vval[:, slot], uval[:, slot], ACT.Tanh).then_inc(s["v_ready"], 1)
                act.wait_ge(s["v_ready"], z + 3)
                act.wait_ge(s["v_free"], z + 1)
                act.wait_ge(s["oh_used"], 4 * z + 4 + 4)
                a.copy(vsplit[:, slot, :, 0, :], vval[:, slot]).then_inc(s["hi_ready"], 1)

            def copy_pairs(i8, first):
                for k in range(8):
                    t = 8 * i8 + k
                    act.wait_ge(s["pairT_ps"], t + 1 + GS)
                    act.wait_ge(s["g_ps"], t + 1)
                    a.copy(pairT[:, k % 4, :], ps[:, 7, 0:T]).then_inc(s["pairT_ready"], 1)
                    if k == 1 and not first:
                        messages(2 * i8 - 1, 1)
                    if k == 5:
                        messages(2 * i8, 0)

            copy_pairs(0, True)
            with act.Fori(1, NCH // 8) as i8:
                copy_pairs(i8, False)
            messages(NCH // 4 - 1, 1)
            act.wait_ge(s["near_done"], 1)
            a.copy(msum[:, 0:NEAR].rearrange("p (b d) -> p b d", b=5), ps[:, 0:5, 0:500]).then_inc(s["near_copied"], 1)
            act.wait_ge(s["sum_done"], 1)
            a.copy(msum[:, NEAR:3000], ps[:, 5, 0:500])
            a.copy(msum[:, 3000:N], ps[:, 6, 0:T]).then_inc(s["sum_copied"], 1)
            layernorm_std(4)

        @block.vector
        def _(dve):
            v = nc.vector
            links = [0]

            def link(ins):
                links[0] += 1
                ins.then_inc(chain, 1)
                dve.wait_ge(chain, links[0])

            dve.wait_ge(ld_edges, 32)
            v.tensor_copy(flt_src, raw_src).then_inc(idx_float, 1)
            v.tensor_copy(flt_dst, raw_dst).then_inc(idx_float, 1)
            dve.wait_ge(idx_float, 2)
            v.tensor_reduce(chunk_lim[:, 0, :], flt_dst, X_AXIS, ALU.max)
            v.tensor_reduce(chunk_lim[:, 1, :], flt_dst, X_AXIS, ALU.min).then_inc(lim_ready, 1)
            dve.wait_ge(ids_ps, 1)
            v.tensor_copy(edge_ids[:].rearrange("p s (b c) -> p (s b) c", b=2), ps[0:T, 0:4, 0:400]).then_inc(ids_ready, 1)
            dve.wait_ge(lims_ps, 1)
            dve.wait_ge(consts, 9)
            for b in range(2):
                v.tensor_reduce(gmax[:, b * 200:b * 200 + 200], ps[0:NT, 4 + b, 0:400].rearrange("p (g c) -> p g c", c=2), X_AXIS, ALU.max)
                i = v.tensor_reduce(gmin[:, b * 200:b * 200 + 200], ps[0:NT, 6 + b, 0:400].rearrange("p (g c) -> p g c", c=2), X_AXIS, ALU.min)
            link(i)
            link(v.tensor_scalar(wcol[:, 1:2], wcol[:, 0:1], float(T - 1), None, ALU.add))
            link(v.scalar_tensor_tensor(tmpg, gmax, wcol[:, 0:1], rev, ALU.is_ge, ALU.mult))
            link(v.tensor_reduce(wcol[:, 2:3], tmpg, X_AXIS, ALU.max))
            link(v.tensor_scalar(wcol[:, 3:4], wcol[:, 2:3], -1.0, float(NG), ALU.mult, ALU.add))
            link(v.tensor_scalar(wcol[:, 3:4], wcol[:, 3:4], float(NG - 1), None, ALU.min))
            link(v.scalar_tensor_tensor(tmpg, gmin, wcol[:, 1:2], fwd, ALU.is_le, ALU.mult))
            link(v.tensor_reduce(wcol[:, 4:5], tmpg, X_AXIS, ALU.max))
            link(v.tensor_tensor(wcol[:, 5:6], wcol[:, 4:5], wcol[:, 3:4], ALU.subtract))
            link(v.tensor_scalar(wcol[:, 5:6], wcol[:, 5:6], 1.0, None, ALU.max))
            v.nop().then_inc(range_cols, 1)
            dve.wait_ge(base_ps, 1)
            link(v.tensor_copy(wcol[:, 6:7], ps[0:NT, 0, 0:1]))
            link(v.tensor_tensor(wcol[:, 7:8], wcol[:, 6:7], wcol[:, 5:6], ALU.add))
            link(v.tensor_tensor(wcol[:, 8:9], wcol[:, 6:7], wcol[:, 3:4], ALU.subtract))
            v.nop().then_inc(tabc_ready, 1)
            dve.wait_ge(tab_ps, 1)
            v.tensor_copy(table[:], ps[0:1, 1, 0:3 * NT]).then_inc(tab_ready, 1)
            dve.wait_ge(tab_ready, 1)
            dve.wait_ge(iotas, 2)
            dve.wait_ge(eids, 1)
            dve.wait_ge(ids_ready, 1)
            dve.sem_inc(oh_used, PAIR)
            with dve.Fori(0, NT) as w:
                k0, k1, back = (tab_load(dve, i, w) for i in range(3))
                dve.wait_ge(last_turned, w + 1)
                v.memset(lastmax, 0.0).then_inc(last_chain, 1)
                with dve.Fori(k0, k1) as k:
                    g = dve.snap(nc.s_assert_within(k - back, 0, NG - 1, skip_runtime_bounds_check_because="a window's steps lie in 0 to NG"))
                    for c in range(PAIR):
                        dve.wait_ge(oh_used, k * PAIR + c + 1)
                        v.tensor_scalar(onehot_dst[:, c, :], iota[:, ds(w * T, T)], edge_ids[:, 1, ds(g * PAIR + c, 1)],
                                        None, ALU.is_equal).then_inc(ohd_built, 1)
                        v.tensor_scalar(onehot_src[:, c, :], iota, edge_ids[:, 0, ds(g * PAIR + c, 1)],
                                        None, ALU.is_equal).then_inc(oh_ready, 1)
                        dve.wait_ge(ohd_built, k * PAIR + c + 1)
                        dve.wait_ge(last_chain, k * PAIR + w + c + 1)
                        v.scalar_tensor_tensor(lastmax, onehot_dst[:, c, :], eid[:, ds(g * PAIR + c, 1)], lastmax,
                                               ALU.mult, ALU.max).then_inc(last_chain, 1)
                dve.wait_ge(adj_summed, w + 1)
                v.tensor_copy(adj3[:, 16:24, ds(w * T, T)].rearrange("p (b j) d -> p b j d", b=2),
                              ps[0:T, 4:6, 0:500].rearrange("p b (j d) -> p b j d", j=4))
                v.tensor_copy(adj3[:, 24, ds(w * T, T)], ps[0:T, 6, 0:T]).then_inc(adj_by_dve, 1)
                dve.wait_ge(last_turned, w + 2)
                v.tensor_reduce(last_edge[:, ds(w, 1)], ps[0:T, 7, 0:T], X_AXIS, ALU.max).then_inc(last_col, 1)
            dve.wait_ge(last_col, NT + 1)
            link(v.tensor_scalar(small[0:T, 0:NT], last_edge[:], -1.0, 0.0, ALU.add, ALU.max))
            v.tensor_copy(eidx, small[0:T, 0:NT]).then_inc(eidx_ready, 1)
            link(v.tensor_scalar(small[0:T, NT:2 * NT], last_edge[:], 1.0, None, ALU.min))
            has = small[0:T, NT:2 * NT].unsqueeze(2)
            dve.wait_ge(ea_ready, 16 * NT)
            v.tensor_copy(eaug[:, :, 16:17], has)
            v.tensor_tensor(eaug[:, :, 0:16], ea, has.to_broadcast([T, NT, 16]), ALU.mult).then_inc(eaug_ready, 1)

            def sage_layer(k):
                s, c = sage, sage_before(k)
                for b in range(NB):
                    dve.wait_ge(s["root_ps"], c["root_ps"] + b + 1)
                    v.tensor_tensor(res[:, b * BT:b * BT + BT, :], ps[0:T, 2, 0:BT * D].rearrange("p (i c) -> p i c", i=BT),
                                    X[:, b * BT:b * BT + BT, 0:D], ALU.add).then_inc(s["root_added"], 1)
                dve.wait_ge(s["root_added"], c["root_added"] + NB)
                with dve.Fori(0, NB) as b:
                    dve.wait_ge(s["proj_ps"], c["proj_ps"] + b + 1)
                    done = c["proj_used"] + 3 * b
                    deg, inv = small[0:T, 0:BT], small[0:T, 8:8 + BT]
                    proj = ps[0:T, 6:8, 0:3 * 129].rearrange("p b (i c) -> p b i c", i=3)
                    v.tensor_scalar(deg[:, 0:3].unsqueeze(2), proj[:, 0, :, 128:129], 1.0, None, ALU.max)
                    v.tensor_scalar(deg[:, 3:BT].unsqueeze(2), proj[:, 1, 0:2, 128:129], 1.0, None, ALU.max).then_inc(s["proj_used"], 1)
                    dve.wait_ge(s["proj_used"], done + 1)
                    v.reciprocal(inv, deg).then_inc(s["proj_used"], 1)
                    dve.wait_ge(s["proj_used"], done + 2)
                    for i in range(BT):
                        tile = res[:, ds(b * BT + i, 1), :].rearrange("p a c -> p (a c)")
                        last = v.scalar_tensor_tensor(tile, proj[:, i // 3, i % 3, 0:D], inv[:, i:i + 1], tile, ALU.mult, ALU.add)
                    last.then_inc(s["proj_used"], 1)
                dve.wait_ge(s["proj_used"], c["proj_used"] + 3 * NB)

            def layernorm(k):
                mean, var, std = (rflat[0:T, i:i + NT] for i in (0, 25, 50))
                link(v.tensor_reduce(mean, res, X_AXIS, ALU.add))
                link(v.tensor_scalar(mean, mean, 1.0 / D, None, ALU.mult))
                link(v.tensor_tensor(res, res, mean.unsqueeze(2).to_broadcast([T, NT, D]), ALU.subtract))
                sq = scratch[0:T, 0:NT * D].rearrange("p (j c) -> p j c", j=NT)
                link(v.tensor_tensor(sq, res, res, ALU.mult))
                link(v.tensor_reduce(var, sq, X_AXIS, ALU.add))
                link(v.tensor_scalar(var, var, 1.0 / D, EPS, ALU.mult, ALU.add))
                v.nop().then_inc(x_var, 1)
                dve.wait_ge(x_std, k)
                link(v.reciprocal(std, std))
                link(v.tensor_tensor(X[:, :, 0:D], res, std.unsqueeze(2).to_broadcast([T, NT, D]), ALU.mult))

            def self_loops(op):
                for j in range(NT):
                    d = adj3[:, j, j * T:j * T + T]
                    i = v.tensor_tensor(d, d, ident[0:T, 0:T], op)
                link(i)

            sage_layer(0)
            layernorm(1)
            v.nop().then_inc(x_ready, 1)
            self_loops(ALU.add)
            for li, (n, fin, heads, fo) in enumerate(GAT):
                s, c = gat, gat_before(li)
                wn = heads * fo
                if n == "a":
                    v.memset(wbuf[D:D + 1, 0:wn], 0.0)
                dve.wait_ge(s["ld"], c["ld"] + 16 * 4)
                for i in range(2):
                    prodw = scratch[0:fin, 1024:1024 + wn]
                    link(v.tensor_tensor(prodw, wbuf[0:fin, 0:wn], scratch[0:fin, 512 * i:512 * i + wn], ALU.mult))
                    link(v.tensor_reduce(small[0:fin, i * heads:(i + 1) * heads], prodw.rearrange("p (h c) -> p h c", h=heads), X_AXIS, ALU.add))
                v.nop().then_inc(s["v_ready"], 1)
                H2 = 2 * heads
                dve.wait_ge(s["att_ps"], c["att_ps"] + 1)
                link(v.tensor_copy(att[:, :, 0:H2], ps[0:T, 7, 0:NT * H2].rearrange("p (j h) -> p j h", j=NT)))
                a_src, a_dst = att[:, :, 0:heads], att[:, :, heads:H2]
                if n == "c":
                    v.memset(h3[:, :, D:D + 1], 1.0).then_inc(s["att_ready"], 1)
                link(v.tensor_reduce(small[0:T, 8:8 + heads], a_src.rearrange("p j h -> p h j"), X_AXIS, ALU.max))
                link(v.tensor_reduce(small[0:T, 8 + heads:8 + H2], a_src.rearrange("p j h -> p h j"), X_AXIS, ALU.min))
                link(v.tensor_scalar(small[0:T, 8 + heads:8 + H2], small[0:T, 8 + heads:8 + H2], -1.0, None, ALU.mult))
                v.nop().then_inc(s["lim_cols"], 1)
                dve.wait_ge(s["lim_ps"], c["lim_ps"] + 1)
                link(v.tensor_reduce(small[0:H2, 16:17], ps[0:H2, 6, 0:T], X_AXIS, ALU.max))
                v.nop().then_inc(s["lim_rows"], 1)
                dve.wait_ge(s["lim_all"], c["lim_all"] + 1)
                link(v.tensor_copy(small[0:T, 20:20 + H2], ps[0:T, 5, 0:H2]))
                top, nbot = small[0:T, 20:20 + heads], small[0:T, 20 + heads:20 + H2]
                rng, inv = small[0:T, 28:28 + heads], small[0:T, 32:32 + heads]
                link(v.tensor_tensor(rng, top, nbot, ALU.add))
                link(v.tensor_scalar(inv, rng, 1e-30, None, ALU.max))
                link(v.reciprocal(inv, inv))

                def by_head(c):
                    return c.unsqueeze(1).to_broadcast([T, NT, heads])

                A, asn, s02, s08 = (cols[:, i, :, 0:heads] for i in range(4))
                link(v.tensor_tensor(asn, a_src, by_head(nbot), ALU.add))
                link(v.tensor_tensor(asn, asn, by_head(inv), ALU.mult))
                link(v.tensor_scalar(asn, asn, 1.0, None, ALU.min))
                dve.wait_ge(s["att_ps"], c["att_ps"] + 1)
                with dve.Fori(0, heads) as h:
                    dve.wait_ge(s["seen_turned"], c["seen_turned"] + h)
                    v.tensor_scalar(seen, adj3[:, 0, :], asn[:, 0, ds(h, 1)], None, ALU.min).then_inc(s["seen_step"], 1)
                    for j in range(1, NT):
                        dve.wait_ge(s["seen_step"], c["seen_step"] + h * NT + j)
                        v.scalar_tensor_tensor(seen, adj3[:, j, :], asn[:, j, ds(h, 1)], seen, ALU.min, ALU.max).then_inc(s["seen_step"], 1)
                    dve.wait_ge(s["seen_turned"], c["seen_turned"] + h + 1)
                    v.tensor_reduce(A[:, 0:24, ds(h, 1)].rearrange("p (b j) h -> p b (j h)", b=6),
                                    ps[0:T, 0:6, 0:500].rearrange("p b (j e) -> p b j e", j=4), X_AXIS, ALU.max)
                    v.tensor_reduce(A[:, 24, ds(h, 1)], ps[0:T, 6, 0:T], X_AXIS, ALU.max).then_inc(s["seen_max"], 1)
                dve.wait_ge(s["seen_max"], c["seen_max"] + heads)
                link(v.tensor_tensor(A, A, by_head(rng), ALU.mult))
                link(v.tensor_tensor(A, A, by_head(nbot), ALU.subtract))
                link(v.tensor_tensor(A, A, a_dst, ALU.add))
                link(v.scalar_tensor_tensor(A, A, NEG, A, ALU.mult, ALU.max))
                r1, r2 = (dst_cols[:, r, 0:NT * heads].rearrange("p (b h i) -> p b i h", b=NB, h=heads) for r in range(2))

                def by_block(x):
                    return x.rearrange("p (b i) h -> p b i h", b=NB)

                v.tensor_tensor(r1, by_block(a_dst), by_block(A), ALU.subtract)
                link(v.tensor_scalar(asn, a_dst, NEG, None, ALU.mult))
                v.tensor_tensor(r2, by_block(asn), by_block(A), ALU.subtract)
                v.memset(dst_cols[:, :, NT * heads:NT * heads + BT], 0.0)
                link(v.tensor_scalar(s02, a_src, NEG, None, ALU.mult))
                link(v.tensor_scalar(s08, a_src, 1.0 - NEG, None, ALU.mult))
                v.nop().then_inc(s["cols_ready"], 1)
                dve.sem_inc(s["tile_used"], SLOTS)

                def copy_row2(p):
                    dve.wait_ge(s["row_ps"], c["row_ps"] + 2 * p + 2)
                    dve.wait_ge(s["shifted"], c["shifted"] + p * NT)
                    v.tensor_copy(rows[0:T, 1, 0:3 * T], ps[0:T, 4, 0:3 * T])
                    v.tensor_copy(rows[0:T, 1, 3 * T:BW], ps[0:T, 5, 0:2 * T]).then_inc(s["row2_ready"], 1)

                fin_ = 128 if n == "b" else D
                sums = agg_sums[:, 0:BT * (fin_ + 1)].rearrange("p (i c) -> p i c", i=BT)

                def invert_den(q):
                    dve.wait_ge(s["agg_copied"], c["agg_copied"] + q + 1)
                    v.reciprocal(small[0:T, 40:40 + BT].unsqueeze(2), sums[:, :, fin_:fin_ + 1]).then_inc(s["den_ready"], 1)

                def add_head(b, q):
                    dve.wait_ge(s["proj_ps"], c["proj_ps"] + q + 1)
                    proj = ps[0:T, 6:8, 0:3 * 129].rearrange("p b (i c) -> p b i c", i=3)
                    v.reciprocal(small[0:T, 40:43].unsqueeze(2), proj[:, 0, :, 128:129])
                    v.reciprocal(small[0:T, 43:45].unsqueeze(2), proj[:, 1, 0:2, 128:129]).then_inc(s["den_ready"], 1)
                    dve.wait_ge(s["den_ready"], c["den_ready"] + q + 1)
                    dve.wait_ge(s["scaled"], c["scaled"] + q)
                    dve.wait_ge(s["acc_zero"], c["acc_zero"] + b + 1)
                    for i in range(BT):
                        last = v.scalar_tensor_tensor(acc[:, i, 0:fo], proj[:, i // 3, i % 3, 0:fo], small[0:T, 40 + i:41 + i],
                                                      acc[:, i, 0:fo], ALU.mult, ALU.add)
                    last.then_inc(s["scaled"], 1)

                def weights(b, h, after_first):
                    q = b * heads + h
                    dve.wait_ge(s["row1_ready"], c["row1_ready"] + q + 1)
                    dve.wait_ge(s["row2_ready"], c["row2_ready"] + q + 1)
                    for j in range(NT + 2):
                        if not after_first and n != "b" and j == ZERO_AT:
                            dve.wait_ge(s["block_stored"], c["block_stored"] + b)
                            v.memset(acc, 0.0).then_inc(s["acc_zero"], 1)
                        if after_first and n == "b" and j == DEN_AT:
                            invert_den(q - 1)
                        if after_first and n != "b" and j == NARROW_ADD_AT:
                            add_head(b, q - 1)
                        if j < NT:
                            dve.wait_ge(s["tile_used"], c["tile_used"] + q * NT + j + 1)
                            v.scalar_tensor_tensor(slots[:, j % SLOTS, :], rows[0:T, 0, :], s08[:, j, ds(h, 1)], rows[0:T, 1, :],
                                                   ALU.add, ALU.max).then_inc(s["shifted"], 1)
                        if j == NT:
                            copy_row2(q + 1)
                        m = j - 2
                        if m >= 0 and m % SLOTS not in POOL_SLOTS[n]:
                            dve.wait_ge(s["exped"], c["exped"] + q * NT + m + 1)
                            v.tensor_tensor(slots[:, m % SLOTS, :], slots[:, m % SLOTS, :], adj3[:, m, ds(b * BW, BW)],
                                            ALU.mult).then_inc(s["tile_by_dve"], 1)

                copy_row2(0)
                with dve.Fori(0, NB) as b:
                    weights(b, 0, False)
                    if heads > 1:
                        with dve.Fori(1, heads) as h:
                            weights(b, h, True)
                    bias = wbuf[0:T, 512:512 + fo].unsqueeze(1).to_broadcast([T, BT, fo])
                    if n == "b":
                        invert_den(b * heads + heads - 1)
                        dve.wait_ge(s["proj_ps"], c["proj_ps"] + (b + 1) * heads)
                        dve.wait_ge(s["tile_by_pool"], c["tile_by_pool"] + (b + 1) * heads * POOL_TILES[n])
                        dve.wait_ge(s["block_stored"], c["block_stored"] + b)
                        for bank, i0, i1 in ((6, 0, 4), (7, 4, BT)):
                            i = v.scalar_tensor_tensor(acc[:, i0:i1, :], ps[0:T, bank, 0:(i1 - i0) * fo].rearrange("p (i c) -> p i c", i=i1 - i0),
                                                       1.0 / heads, bias[:, i0:i1, :], ALU.mult, ALU.add)
                    else:
                        add_head(b, b * heads + heads - 1)
                        dve.wait_ge(s["scaled"], c["scaled"] + (b + 1) * heads)
                        i = v.scalar_tensor_tensor(acc[:, :, 0:fo], acc[:, :, 0:fo], 1.0 / heads, bias, ALU.mult, ALU.add)
                    i.then_inc(s["block_ready"], 1)
                dve.wait_ge(s["back"], c["back"] + 16)
                if n != "c":
                    t, tc = bn, bn_before(li)
                    gam, bet, mu, var, std = (rflat[0:T, i * 128:i * 128 + 128] for i in range(5))
                    hid_f = hid[:, :, 0:128]
                    dve.wait_ge(t["ld"], tc["ld"] + 32)

                    def row(c):
                        return c.unsqueeze(1).to_broadcast([T, NT, 128])

                    dve.wait_ge(t["sum_ps"], tc["sum_ps"] + 1)
                    link(v.tensor_scalar(mu, ps[0:T, 0, 0:128], 1.0 / N, None, ALU.mult))
                    link(v.tensor_tensor(hid_f, hid_f, row(mu), ALU.subtract))
                    sq = scratch[0:T, 0:3200].rearrange("p (j c) -> p j c", j=NT)
                    v.tensor_tensor(sq, hid_f, hid_f, ALU.mult).then_inc(t["sq_ready"], 1)
                    dve.wait_ge(t["var_ps"], tc["var_ps"] + 1)
                    v.tensor_scalar(var, ps[0:T, 1, 0:128], 1.0 / N, EPS, ALU.mult, ALU.add).then_inc(t["var_ready"], 1)
                    dve.wait_ge(t["std_ready"], tc["std_ready"] + 1)
                    link(v.reciprocal(std, std))
                    link(v.tensor_tensor(std, std, gam, ALU.mult))
                    link(v.tensor_tensor(hid_f, hid_f, row(std), ALU.mult))
                    link(v.tensor_tensor(hid_f, hid_f, row(bet), ALU.add))
                    v.tensor_scalar(sq, hid_f, 0.0, None, ALU.min).then_inc(t["min_ready"], 1)
                    dve.wait_ge(t["exp_ready"], tc["exp_ready"] + 1)
                    link(v.tensor_scalar(sq, sq, -1.0, None, ALU.add))
                    v.memset(hid[:, :, 128:129], 1.0)
                    v.scalar_tensor_tensor(hid_f, hid_f, 0.0, sq, ALU.max, ALU.add).then_inc(t["hid_ready"], 1)
                    dve.wait_ge(t["hid_ready"], tc["hid_ready"] + 1)
            g3 = scratch[0:T, 0:NT * D].rearrange("p (j c) -> p j c", j=NT)
            link(v.tensor_tensor(res, g3, X[:, :, 0:D], ALU.add))
            layernorm(2)
            v.nop().then_inc(x_ready, 1)
            self_loops(ALU.subtract)
            sage_layer(1)
            layernorm(3)
            v.nop().then_inc(x_ready, 1)
            s = m3
            dve.wait_ge(s["ld"], 16 * 12)
            v.memset(src3[:, 0:LAG], 0.0)
            v.tensor_copy(src3[:, LAG:], idx3[:, 0, :]).then_inc(s["src_ready"], 1)
            link(v.tensor_tensor(small[:, 0:D], ident[:, 0:D], ident[:, D:2 * D], ALU.add))
            v.nop().then_inc(s["sel_ready"], 1)
            dve.sem_inc(s["g_ps"], 4)
            dve.sem_inc(s["prod_ready"], 1)
            dve.sem_inc(s["lo_ready"], 2)
            dve.sem_inc(s["oh_used"], 4)
            dve.wait_ge(s["src_ready"], 1)
            dve.wait_ge(s["iota"], 1)

            def onehot_near(col, slot):
                dve.wait_ge(s["oh_used"], col + 1)
                v.tensor_scalar(oh3[:, slot, 0:NEAR], iota3[:, 0:NEAR], src3[:, ds(col, 1)], None, ALU.is_equal).then_inc(s["oh_ready"], 1)

            for col in range(4):
                onehot_near(col, col)
            with dve.Fori(0, NCH // 8) as i8:
                for pair in range(4):
                    k = 2 * pair
                    t = 8 * i8 + k
                    u = 4 * i8 + pair
                    dve.wait_ge(s["g_ps"], t + 2 + 4)
                    dve.wait_ge(s["u_ready"], u + 1)
                    v.tensor_tensor(prod[:, :, 0:8, :], ps[0:T, 5:7, :].rearrange("p s (b c) -> p s b c", b=8),
                                    basis[:, ds(t, 2), :].unsqueeze(3).to_broadcast([T, 2, 8, D]),
                                    ALU.mult).then_inc(s["prod_ready"], 1)
                    dve.wait_ge(s["prod_ready"], u + 2)
                    if k % 4 == 0:
                        dve.wait_ge(s["v_ready"], 2 * i8 + k // 4 + 1)
                    v.tensor_reduce(uval[:, k // 4, k % 4:k % 4 + 2, :], prod[:].rearrange("p s b c -> p s c b"), X_AXIS, ALU.add).then_inc(s["u_ready"], 1)
                    for c in range(2):
                        onehot_near(t + 4 + c, (k + c) % 4)
                    if k % 4 == 2:
                        z = 2 * i8 + k // 4
                        dve.wait_ge(s["hi_ready"], z + 1)
                        v.tensor_tensor(vsplit[:, k // 4, :, 1, :], vval[:, k // 4], vsplit[:, k // 4, :, 0, :], ALU.subtract).then_inc(s["lo_ready"], 1)
            for col in range(NCH + 4, NCH + LAG):
                onehot_near(col, col % 4)
            dve.wait_ge(s["oh_used"], NCH + LAG + 4)
            with dve.Fori(0, NCH // 16) as i16:
                for k in range(16):
                    dve.wait_ge(s["far_oh_used"], 16 * i16 + k + 13)
                    v.tensor_scalar(oh3[:, k % 4, 0:N - NEAR], iota3[:, NEAR:N], src3[:, ds(16 * i16 + k + LAG, 1)], None, ALU.is_equal).then_inc(s["far_oh_ready"], 1)
            dve.wait_ge(s["turned"], 1)
            for b in range(4):
                n8 = 8 if b < 3 else 1
                i = v.scalar_tensor_tensor(res[:, b * 8:b * 8 + n8, :], X[:, b * 8:b * 8 + n8, 0:D], 2.0,
                                           ps[0:T, b, 0:n8 * D].rearrange("p (j c) -> p j c", j=n8), ALU.mult, ALU.add)
            link(i)
            layernorm(4)
            v.nop().then_inc(x_ready, 1)

        @block.tensor
        def _(pe):
            t_ = nc.tensor

            def mm(o_, l, r, start=True, stop=True, skip=False):
                return t_.matmul(o_, l, r, start=start, stop=stop, skip_group_check=skip)

            I = ident
            pe.wait_ge(idx_float, 2)
            pe.wait_ge(consts, 9)
            for s_, f in enumerate((flt_src, flt_dst)):
                for k in range(8):
                    i = t_.transpose(ps[0:T, 2 * s_ + k // 4, (k % 4) * 100:(k % 4) * 100 + 100], f[:, k, :], I[0:100, 0:100])
            i.then_inc(ids_ps, 1)
            pe.wait_ge(lim_ready, 1)
            for m in range(2):
                for k in range(8):
                    i = mm(ps[0:NT, 4 + 2 * m + k // 4, (k % 4) * 100:(k % 4) * 100 + 100],
                           chunk_lim[:, m, k:k + 1].to_broadcast([100, NT]), I[0:100, 0:100])
            i.then_inc(lims_ps, 1)
            pe.wait_ge(range_cols, 1)
            pe.wait_ge(ids_ready, 1)
            mm(ps[0:NT, 0, 0:1], lower, wcol[:, 5:6]).then_inc(base_ps, 1)
            pe.wait_ge(tabc_ready, 1)
            for m in range(3):
                i = mm(ps[0:1, 1, m * NT:m * NT + NT], wcol[:, 6 + m:7 + m], I[0:NT, 0:NT])
            i.then_inc(tab_ps, 1)
            pe.wait_ge(tab_ready, 1)
            pe.wait_ge(iotas, 2)

            def open_banks():
                for b in range(BANKS):
                    mm(ps[0:T, b, 0:4], zeros[:, 0:T], zeros[:, 0:4], True, False, True)

            with pe.Fori(0, NT) as w:
                k0, k1 = (tab_load(pe, i, w) for i in range(2))
                pe.wait_ge(adj_by_act, w + 1)
                pe.wait_ge(adj_by_dve, w + 1)
                open_banks()
                with pe.Fori(k0, k1) as k:
                    for c in range(PAIR):
                        pe.wait_ge(oh_ready, k * PAIR + c + 1)
                        for j in range(NT):
                            b, c0 = bank_cols(j)
                            i = mm(ps[0:T, b, c0:c0 + T], onehot_src[:, c, j * T:j * T + T], onehot_dst[:, c, :], False, False, True)
                        i.then_inc(oh_used, 1)
                mm(ps[0:T, 6, 0:4], zeros[:, 0:T], zeros[:, 0:4], False, True, True).then_inc(adj_summed, 1)
                pe.wait_ge(last_chain, w + k1 * PAIR + 1)
                pe.wait_ge(last_col, w + 1)
                t_.transpose(ps[0:T, 7, 0:T], lastmax, I[0:T, 0:T]).then_inc(last_turned, 1)

            def transpose_nodes(s, feat, fin):
                for j in range(NT):
                    b, c0 = bank_cols(j)
                    i_ = t_.transpose(ps[0:fin, b, c0:c0 + T], feat[:, j, 0:fin], I[0:T, 0:T])
                i_.then_inc(s["ft_ps"], 1)

            def sage_layer(k):
                s, c = sage, sage_before(k)
                transpose_nodes(s, X, D)
                pe.wait_ge(s["ft_ready"], c["ft_ready"] + 1)
                if k == 0:
                    pe.wait_ge(eaug_ready, 1)
                    pe.wait_ge(ld_w0, 16 * 5)
                else:
                    pe.wait_ge(s["ld"], c["ld"] + 16 * 3)
                for b in range(NB):
                    pe.wait_ge(s["root_added"], c["root_added"] + b)
                    if k == 0:
                        for i in range(BT):
                            bank, c0 = block_cols(i)
                            last = t_.transpose(ps[0:17, bank, c0:c0 + T], eaug[:, b * BT + i, :], I[0:T, 0:T])
                        last.then_inc(s["et_ps"], 1)
                        pe.wait_ge(s["et_ready"], c["et_ready"] + b + 1)
                    for i in range(BT):
                        j = b * BT + i
                        o_ = ps[0:T, 2, i * D:i * D + D]
                        mm(o_, ft[0:D, j * T:j * T + T], wbuf[0:D, 64:128], True, False)
                        if k == 0:
                            mm(o_, aggT[0:17, i * T:i * T + T], wbuf[0:17, 128:192], False, False)
                        last = mm(o_, ones[0:1, 0:T], wbuf[0:1, 192:256], False, True)
                    last.then_inc(s["root_ps"], 1)
                pe.sem_inc(s["tile_used"], SLOTS)
                with pe.Fori(0, NB) as b:
                    pe.wait_ge(s["agg_out"], c["agg_out"] + b)
                    for j in range(NT):
                        pe.wait_ge(s["tile_ready"], c["tile_ready"] + b * NT + j + 1)
                        for bank, c0, n_ in PIECES:
                            last = mm(ps[0:D + 1, bank, 0:n_], X[:, j, :], slots[:, j % SLOTS, c0:c0 + n_], j == 0, j == NT - 1)
                        last.then_inc(s["tile_used"], 1)
                    pe.wait_ge(s["agg_out"], c["agg_out"] + b + 1)
                    pe.wait_ge(s["proj_used"], c["proj_used"] + 3 * b)
                    for i in range(BT):
                        o_ = ps[0:T, 6 + i // 3, (i % 3) * 129:(i % 3) * 129 + 129]
                        mm(o_[:, 0:D], aggT[0:D, i * T:i * T + T], wbuf[0:D, 0:64])
                        last = mm(o_[:, 128:129], aggT[0:D + 1, i * T:i * T + T], I[0:D + 1, D:D + 1])
                    last.then_inc(s["proj_ps"], 1)

            pe.wait_ge(ld_x, 16)
            pe.wait_ge(adj_by_act, NT + 1)
            pe.wait_ge(adj_by_dve, NT + 1)
            pe.wait_ge(last_col, NT + 1)
            sage_layer(0)
            for li, (n, fin, heads, fo) in enumerate(GAT):
                s, c = gat, gat_before(li)
                H2 = 2 * heads
                if li == 0:
                    pe.wait_ge(x_ready, 1)
                else:
                    pe.wait_ge(bn["hid_ready"], li)
                transpose_nodes(s, X if n == "a" else hid, fin)
                pe.wait_ge(s["v_ready"], c["v_ready"] + 1)
                pe.wait_ge(s["ft_ready"], c["ft_ready"] + 1)
                for j in range(NT):
                    l = ft[0:fin, j * T:j * T + T]
                    if n == "c":
                        mm(ps[0:T, j // 8, (j % 8) * D:(j % 8) * D + D], l, wbuf[0:fin, 0:D])
                    last = mm(ps[0:T, 7, j * H2:j * H2 + H2], l, small[0:fin, 0:H2])
                last.then_inc(s["att_ps"], 1)
                pe.wait_ge(s["lim_cols"], c["lim_cols"] + 1)
                t_.transpose(ps[0:H2, 6, 0:T], small[0:T, 8:8 + H2], I[0:T, 0:T]).then_inc(s["lim_ps"], 1)
                pe.wait_ge(s["lim_rows"], c["lim_rows"] + 1)
                mm(ps[0:T, 5, 0:H2], small[0:H2, 16:17].to_broadcast([H2, T]), I[0:H2, 0:H2]).then_inc(s["lim_all"], 1)
                if n == "c":
                    pe.wait_ge(s["att_ready"], c["att_ready"] + 2)
                with pe.Fori(0, heads) as h:
                    pe.wait_ge(s["seen_step"], c["seen_step"] + (h + 1) * NT)
                    pe.wait_ge(s["seen_max"], c["seen_max"] + h)
                    for j in range(NT):
                        b, c0 = bank_cols(j)
                        last = t_.transpose(ps[0:T, b, c0:c0 + T], seen[:, j * T:j * T + T], I[0:T, 0:T])
                    last.then_inc(s["seen_turned"], 1)
                pe.wait_ge(s["cols_ready"], c["cols_ready"] + 1)
                feat = {"a": X, "b": hid, "c": h3}[n]
                fin_ = 128 if n == "b" else D
                F1 = fin_ + 1

                def broadcast_row(p, r):
                    pe.wait_ge(s["diag_ready"], c["diag_ready"] + 2 * p + r + 1)
                    pe.wait_ge(s[("row1_ready", "row2_ready")[r]], c["row1_ready"] + p)
                    for i in range(BT):
                        bank, c0 = block_cols(i)
                        last = mm(ps[0:T, 2 + 2 * r + bank, c0:c0 + T], ones[0:T, 0:T], diag[:, i, :])
                    last.then_inc(s["row_ps"], 1)

                def turn_sums(q, rows_copied):
                    pe.wait_ge(s["row2_ready"], c["row2_ready"] + rows_copied)
                    pe.wait_ge(s["scaled"], c["scaled"] + q + 1)
                    for i in range(BT):
                        bank, c0 = block_cols(i)
                        k_ = min(F1, 128)
                        last = t_.transpose(ps[0:k_, 4 + bank, c0:c0 + T], agg_sums[:, i * F1:i * F1 + k_], I[0:T, 0:T])
                    last.then_inc(s["aggT_ps"], 1)

                def project(q, h):
                    if n == "b":
                        pe.wait_ge(s["aggT_ready"], c["aggT_ready"] + q + 1)
                        for i in range(BT):
                            last = mm(ps[0:T, 6 + i // 4, (i % 4) * fo:(i % 4) * fo + fo], aggT[:, i * T:i * T + T],
                                      wbuf[:, ds(h * 128, 128)], False, False, True)
                        last.then_inc(s["proj_ps"], 1)
                        return
                    pe.wait_ge(s["agg_copied"], c["agg_copied"] + q + 1)
                    pe.wait_ge(s["scaled"], c["scaled"] + q)
                    for i in range(BT):
                        o_ = ps[0:T, 6 + i // 3, (i % 3) * 129:(i % 3) * 129 + 129]
                        w_ = I[0:D, 0:D] if n == "c" else wbuf[0:D + 1, ds(h * 128, 128)]
                        mm(o_[:, 0:fo], aggT[0:D if n == "c" else D + 1, i * T:i * T + T], w_)
                        last = mm(o_[:, 128:129], aggT[0:D + 1, i * T:i * T + T], I[0:D + 1, D:D + 1])
                    last.then_inc(s["proj_ps"], 1)

                def sum_tiles(b, h, after_first):
                    q = b * heads + h
                    pe.wait_ge(s["agg_copied"], c["agg_copied"] + q)
                    for j in range(NT):
                        if j % SLOTS in POOL_SLOTS[n]:
                            pe.wait_ge(s["tile_by_pool"], c["tile_by_pool"] + q * POOL_TILES[n] + tile_rank(n, j))
                        else:
                            pe.wait_ge(s["tile_by_dve"], c["tile_by_dve"] + q * DVE_TILES[n] + tile_rank(n, j))
                        for bank, c0, n_ in PIECES if n != "b" else ():
                            last = mm(ps[0:D + 1, bank, 0:n_], feat[:, j, :], slots[:, j % SLOTS, c0:c0 + n_], j == 0, j == NT - 1)
                        for i in range(BT) if n == "b" else ():
                            bank, i0 = (0, i) if i < 3 else (1, i - 3)
                            last = mm(ps[0:T, bank, i0 * F1:i0 * F1 + F1], slots[:, j % SLOTS, i * T:i * T + T], feat[:, j, 0:F1],
                                      j == 0 and i0 == 0, j == NT - 1, True)
                        last.then_inc(s["tile_used"], 1)
                        if after_first and n == "b" and j == TURN_AT:
                            turn_sums(q - 1, q + 1)
                        if after_first and j == (PROJ_AT if n == "b" else NARROW_PROJ_AT):
                            project(q - 1, h - 1)
                        if j in ROW_AT:
                            broadcast_row(q + 1, ROW_AT.index(j))

                for r in range(2):
                    broadcast_row(0, r)
                with pe.Fori(0, NB) as b:
                    if n == "b":
                        pe.wait_ge(s["block_ready"], c["block_ready"] + b)
                        mm(ps[0:T, 6, 0:4 * fo], ones[0:1, 0:T], ident[0:1, 1:2].to_broadcast([1, 4 * fo]), True, False, True)
                        mm(ps[0:T, 7, 0:fo], ones[0:1, 0:T], ident[0:1, 1:2].to_broadcast([1, fo]), True, False, True)
                    sum_tiles(b, 0, False)
                    if heads > 1:
                        with pe.Fori(1, heads) as h:
                            sum_tiles(b, h, True)
                    q_last = b * heads + heads - 1
                    if n == "b":
                        turn_sums(q_last, q_last + 2)
                    project(q_last, heads - 1)
                pe.wait_ge(s["row1_ready"], c["row1_ready"] + NB * heads + 1)
                pe.wait_ge(s["row2_ready"], c["row2_ready"] + NB * heads + 1)
                if n != "c":
                    t, tc = bn, bn_before(li)
                    pe.wait_ge(s["back"], c["back"] + 16)
                    for j in range(NT):
                        last = mm(ps[0:T, 0, 0:128], ones[0:T, 0:T], hid[:, j, 0:128], j == 0, j == NT - 1)
                    last.then_inc(t["sum_ps"], 1)
                    pe.wait_ge(t["sq_ready"], tc["sq_ready"] + 1)
                    for j in range(NT):
                        last = mm(ps[0:T, 1, 0:128], ones[0:T, 0:T], scratch[0:T, j * 128:j * 128 + 128], j == 0, j == NT - 1)
                    last.then_inc(t["var_ps"], 1)
            pe.wait_ge(x_ready, 2)
            sage_layer(1)
            s = m3
            pe.wait_ge(x_ready, 3)
            transpose_nodes(s, X, D)
            pe.wait_ge(s["ld"], 16 * 12)
            w2 = w3l[0:D, 256:768].rearrange("p (m b) -> p b m", b=8)
            for b in range(8):
                last = t_.transpose(ps[0:D, 7, b * D:b * D + D], w2[:, b, :], I[0:D, 0:D])
            last.then_inc(s["w2T_ps"], 1)
            pe.wait_ge(s["w2T_ready"], 1)
            for b in range(8):
                last = mm(ps[:, 7, b * D:b * D + D], w2T[:, b, :], w3l[0:D, 192:256])
            last.then_inc(s["wc_ps"], 1)
            pe.wait_ge(s["ft_ready"], 1)
            for b in range(BANKS):
                n_ = 500 if b < 6 else T
                last = mm(ps[0:D, b, 0:n_], w3l[0:D, 0:64], ft[0:D, b * 500:b * 500 + n_])
            last.then_inc(s["p1_ps"], 1)
            pe.wait_ge(s["p1_ready"], 1)
            for j in range(NT):
                o_ = ps[0:T, j // 4, (j % 4) * 128:(j % 4) * 128 + 128]
                mm(o_, p1T[:, j * T:j * T + T], w3l[0:D, 64:192], True, False, True)
                last = mm(o_[:, D:2 * D], ones[0:1, 0:T], w3l[0:1, 896:960], False, True, True)
            last.then_inc(s["qr_ps"], 1)
            pe.wait_ge(s["qr_ready"], 1)
            pe.wait_ge(s["wc_ready"], 1)

            pe.wait_ge(s["iota"], 3)
            pe.sem_inc(s["pairT_ps"], GS)
            pe.sem_inc(s["far_oh_used"], 16)

            def zero_sum(banks, start):
                for b, n_ in banks:
                    i_ = mm(ps[:, b, 0:n_], zero16[:, 0:128], zero16[:, 0:n_], start, not start, True)
                return i_

            def turn_pair(t, i8, k):
                pe.wait_ge(gathered[k], 32 * i8 + 32)
                pe.wait_ge(s["pairT_ready"], t + 1)
                t_.transpose(ps[:, 7, 0:T], gath[:, k, :], I[0:T, 0:T]).then_inc(s["pairT_ps"], 1)

            def parts(t, i8, k):
                pe.wait_ge(s["pairT_ready"], t + 2)
                if k % 2 == 0:
                    pe.wait_ge(s["prod_ready"], 4 * i8 + k // 2 + 1)
                mm(ps[0:T, 5 + k % 2, :], pairT[:, k % 4, :], wc).then_inc(s["g_ps"], 1)

            def add_near(col, z, k):
                pe.wait_ge(s["oh_ready"], col + 1)
                pe.wait_ge(s["lo_ready"], z + 1)
                for b in range(5):
                    last = mm(ps[:, b, 0:500], vsplit[:, k // 4, k % 4, :, :].rearrange("p h c -> p (h c)"), oh3[:, k % 4, b * 500:b * 500 + 500], False, False, True)
                last.then_inc(s["oh_used"], 1)

            near = [(b, 500) for b in range(5)]
            far = [(5, 500), (6, T)]
            zero_sum(near, True)
            with pe.Fori(0, NCH // 8) as i8:
                for k in range(0, 8, 2):
                    t = 8 * i8 + k
                    turn_pair(t, i8, k)
                    add_near(t, 2 * i8 + k // 4, k)
                    turn_pair(t + 1, i8, k + 1)
                    parts(t, i8, k)
                    add_near(t + 1, 2 * i8 + k // 4, k + 1)
                    parts(t + 1, i8, k + 1)
            for k in range(LAG):
                add_near(NCH + k, NCH // 4 + k // 4, k)
            zero_sum(near, False).then_inc(s["near_done"], 1)
            pe.wait_ge(s["prod_ready"], NCH // 2 + 1)
            zero_sum(far, True)
            with pe.Fori(0, NCH // 16) as i16:
                for k in range(16):
                    if k % 4 == 0:
                        pe.wait_ge(v_loaded[k // 4], 16 * i16 + 16)
                    pe.wait_ge(s["far_oh_ready"], 16 * i16 + k + 1)
                    for b, n_ in far:
                        last = mm(ps[:, b, 0:n_], vin[:, k // 4, k % 4, :], oh3[:, k % 4, (b - 5) * 500:(b - 5) * 500 + n_], False, False, True)
                    last.then_inc(s["far_oh_used"], 1)
            zero_sum(far, False).then_inc(s["sum_done"], 1)
            pe.wait_ge(s["near_copied"], 1)
            pe.wait_ge(s["sum_copied"], 1)
            pe.wait_ge(s["sel_ready"], 1)
            for j in range(NT):
                last = mm(ps[0:T, j // 8, (j % 8) * D:(j % 8) * D + D], msum[:, j * T:j * T + T], small[:, 0:D])
            last.then_inc(s["turned"], 1)


def kernel(**inputs):
    import numpy as np
    import concourse.bacc as bacc
    from concourse.bass_utils import run_bass_kernel_spmd

    nc = bacc.Bacc("TRN2", target_bir_lowering=False, num_devices=1)
    arrays, params = {}, {}
    for name, value in inputs.items():
        a = np.ascontiguousarray(value)
        arrays[f"in_{name}"] = a
        params[name] = nc.dram_tensor(f"in_{name}", a.shape, mybir.dt.from_np(a.dtype), kind="ExternalInput").ap()
    out = nc.dram_tensor("out", (N, D), F32, kind="ExternalOutput").ap()
    build_gnn(nc, params, out)
    got = run_bass_kernel_spmd(nc, [arrays], core_ids=[0])
    return got.results[0]["out"]
```
